# Optimizing a Trainium2 kernel written in Bass

```python
import numpy as np
import jax
import jax.numpy as jnp

def _softmax(x, axis=-1):
    return jax.nn.softmax(x, axis=axis)

def _gelu(x):
    return jax.nn.gelu(x, approximate=True)

def _silu(x):
    return jax.nn.silu(x)

def _sigmoid(x):
    return jax.nn.sigmoid(x)

def _layernorm(x, axis=-1, eps=1e-05):
    m = jnp.mean(x, axis=axis, keepdims=True)
    v = jnp.var(x, axis=axis, keepdims=True)
    return (x - m) / jnp.sqrt(v + eps)

def _scatter_add(tgt, idx, src, axis=0):
    return tgt.at[idx].add(src)

def _segment_sum(src, seg, n):
    return jax.ops.segment_sum(src, seg, n)
kernel_name = 'mk_decoder_postln_d1_seqx_r4_3c7790'

def setup_inputs(seed: int=0):
    np.random.seed(seed)
    _w = jnp.asarray

    def _rec_inputs():
        import jax
        import jax.numpy as jnp
        _rk = jax.random.key(seed)
        x = 7.22e-05 + 1 * jax.random.normal(jax.random.fold_in(_rk, 1), (4, 1024, 256), jnp.float32)
        _lenS = 1024 - jax.random.randint(jax.random.fold_in(_rk, 7), (4,), 0, max(1, 1024 // 4) + 1, jnp.int32)
        _lenS2 = 77 - jax.random.randint(jax.random.fold_in(_rk, 8), (4,), 0, max(1, 77 // 4) + 1, jnp.int32)
        _ctx_768P = jax.random.normal(jax.random.fold_in(_rk, 11), (4, 16, 192), jnp.float32)
        _ctx_768c = jax.random.dirichlet(jax.random.fold_in(_rk, 511), 0.3 * jnp.ones((16,), jnp.float32), (4, 77))
        _ctx_768t = jnp.einsum('bsk,bkd->bsd', _ctx_768c, _ctx_768P)
        _ctx_768t = _ctx_768t * jax.lax.rsqrt(jnp.mean(jnp.square(_ctx_768t)) + 1e-12) * 0.953939
        ctx_768 = 2.09791e-05 + 1.00001 * (_ctx_768t + 0.3 * jax.random.normal(jax.random.fold_in(_rk, 611), (4, 77, 192), jnp.float32))
        _validS = jnp.arange(1024)[None, :] < _lenS[:, None]
        _validS2 = jnp.arange(77)[None, :] < _lenS2[:, None]
        _causal = jnp.tril(jnp.ones((1024, 1024), dtype=bool))
        mask_BxS_bk0 = jnp.logical_not(jnp.broadcast_to(_validS[:, :], (4, 1024)))
        return (x, ctx_768, mask_BxS_bk0)
    x, ctx_768, mask_BxS_bk0 = _rec_inputs()

    def _L0_attn_setup():
        import jax, jax.numpy as jnp
        import numpy as np
        DIM = 256
        HEADS = 16
        HEAD_DIM = DIM // HEADS
        NUM_FILTERS = 4
        NUM_TAPS = 101
        RES = 128

        def _fir_fft(c, sig):
            R = sig.shape[0]
            L = R + c.shape[0] - 1
            out = jnp.fft.ifft(jnp.fft.fft(sig, n=L) * jnp.fft.fft(c, n=L)).real
            return out[:R]
        key = jax.random.key(seed)
        ks = jax.random.split(key, 5)
        B, S = (2, 512)
        x = jax.random.normal(ks[0], (B, S, DIM), dtype=jnp.float32)
        Wqkv = jax.random.normal(ks[1], (3 * DIM, DIM), dtype=jnp.float32) * DIM ** (-0.5)
        Wout = jax.random.normal(ks[2], (DIM, DIM), dtype=jnp.float32) * DIM ** (-0.5)
        Wpos = jax.random.normal(ks[3], (HEADS, NUM_FILTERS), dtype=jnp.float32) * 0.5
        coeffs = jax.random.normal(ks[4], (NUM_FILTERS, NUM_TAPS), dtype=jnp.float32) * 0.05
        return {'x': x, 'Wqkv': Wqkv, 'Wout': Wout, 'Wpos': Wpos, 'coeffs': coeffs}
    _L0_attn_all = _L0_attn_setup()
    _L0_attn_in = {k: v for k, v in _L0_attn_all.items() if k in ('Wqkv', 'Wout', 'Wpos', 'coeffs')}
    del _L0_attn_all

    def _L0_xattn_setup():
        import jax, jax.numpy as jnp
        import numpy as np
        NUM_HEADS = 16
        key = jax.random.key(seed)
        k1, k2, k3, k4, k5 = jax.random.split(key, 5)
        B, N, C = (4, 512, 256)
        N2, Cy = (256, 192)
        x = jax.random.normal(k1, (B, N, C), dtype=jnp.float32)
        y = jax.random.normal(k2, (B, N2, Cy), dtype=jnp.float32)
        pad_mask = jax.random.randint(k3, (B, N), 0, 2).astype(jnp.bool_)
        Wq = jax.random.normal(k4, (C, C), dtype=jnp.float32) * C ** (-0.5)
        Wkv = jax.random.normal(k5, (2 * C, Cy), dtype=jnp.float32) * Cy ** (-0.5)
        return {'x': x, 'y': y, 'pad_mask': pad_mask, 'Wq': Wq, 'Wkv': Wkv}
    _L0_xattn_all = _L0_xattn_setup()
    _L0_xattn_in = {k: v for k, v in _L0_xattn_all.items() if k in ('Wq', 'Wkv')}
    del _L0_xattn_all

    def _L0_ffn_setup():
        import jax, jax.numpy as jnp
        import numpy as np
        DIM = 256
        HID = 512
        E = 8
        K = 2
        R = 16
        B_, S_ = (2, 256)

        def _lora_in(xf, W, b, A, B):
            base = jnp.einsum('td,ehd->teh', xf, W)
            low = jnp.einsum('ter,ehr->teh', jnp.einsum('td,erd->ter', xf, A), B)
            return base + low + b

        def _lora_out(g, W, b, A, B):
            base = jnp.einsum('teh,edh->ted', g, W)
            low = jnp.einsum('ter,edr->ted', jnp.einsum('teh,erh->ter', g, A), B)
            return base + low + b
        key = jax.random.key(seed)
        ks = jax.random.split(key, 14)
        n = lambda k, shape, scale: jax.random.normal(k, shape, jnp.float32) * scale
        inp = {'x': jax.random.normal(ks[0], (B_, S_, DIM), jnp.float32), 'Wg': n(ks[1], (E, DIM), DIM ** (-0.5)), 'W1': n(ks[2], (E, HID, DIM), DIM ** (-0.5)), 'b1': jnp.zeros((E, HID), jnp.float32), 'A1': n(ks[3], (E, R, DIM), DIM ** (-0.5)), 'B1': n(ks[4], (E, HID, R), 0.01), 'W2': n(ks[5], (E, DIM, HID), HID ** (-0.5)), 'b2': jnp.zeros((E, DIM), jnp.float32), 'A2': n(ks[6], (E, R, HID), HID ** (-0.5)), 'B2': n(ks[7], (E, DIM, R), 0.01), 'W3': n(ks[8], (E, HID, DIM), DIM ** (-0.5)), 'b3': jnp.zeros((E, HID), jnp.float32), 'A3': n(ks[9], (E, R, DIM), DIM ** (-0.5)), 'B3': n(ks[10], (E, HID, R), 0.01)}
        return inp
    _L0_ffn_all = _L0_ffn_setup()
    _L0_ffn_in = {k: v for k, v in _L0_ffn_all.items() if k in ('Wg', 'W1', 'b1', 'A1', 'B1', 'W2', 'b2', 'A2', 'B2', 'W3', 'b3', 'A3', 'B3')}
    del _L0_ffn_all
    return {'x': x, 'ctx_768': ctx_768, 'mask_BxS_bk0': mask_BxS_bk0, 'L0_attn_Wqkv': _L0_attn_in['Wqkv'], 'L0_attn_Wout': _L0_attn_in['Wout'], 'L0_attn_Wpos': _L0_attn_in['Wpos'], 'L0_attn_coeffs': _L0_attn_in['coeffs'], 'L0_xattn_Wq': _L0_xattn_in['Wq'], 'L0_xattn_Wkv': _L0_xattn_in['Wkv'], 'L0_ffn_Wg': _L0_ffn_in['Wg'], 'L0_ffn_W1': _L0_ffn_in['W1'], 'L0_ffn_b1': _L0_ffn_in['b1'], 'L0_ffn_A1': _L0_ffn_in['A1'], 'L0_ffn_B1': _L0_ffn_in['B1'], 'L0_ffn_W2': _L0_ffn_in['W2'], 'L0_ffn_b2': _L0_ffn_in['b2'], 'L0_ffn_A2': _L0_ffn_in['A2'], 'L0_ffn_B2': _L0_ffn_in['B2'], 'L0_ffn_W3': _L0_ffn_in['W3'], 'L0_ffn_b3': _L0_ffn_in['b3'], 'L0_ffn_A3': _L0_ffn_in['A3'], 'L0_ffn_B3': _L0_ffn_in['B3']}

def reference(x, ctx_768, mask_BxS_bk0, L0_attn_Wqkv, L0_attn_Wout, L0_attn_Wpos, L0_attn_coeffs, L0_xattn_Wq, L0_xattn_Wkv, L0_ffn_Wg, L0_ffn_W1, L0_ffn_b1, L0_ffn_A1, L0_ffn_B1, L0_ffn_W2, L0_ffn_b2, L0_ffn_A2, L0_ffn_B2, L0_ffn_W3, L0_ffn_b3, L0_ffn_A3, L0_ffn_B3):
    import jax
    import jax.numpy as jnp

    def _L0_attn_ref(x, Wqkv, Wout, Wpos, coeffs):
        import jax, jax.numpy as jnp
        import numpy as np
        DIM = 256
        HEADS = 16
        HEAD_DIM = DIM // HEADS
        NUM_FILTERS = 4
        NUM_TAPS = 101
        RES = 128

        def _fir_fft(c, sig):
            R = sig.shape[0]
            L = R + c.shape[0] - 1
            out = jnp.fft.ifft(jnp.fft.fft(sig, n=L) * jnp.fft.fft(c, n=L)).real
            return out[:R]
        B, S, D = x.shape
        scale = HEAD_DIM ** (-0.5)
        proto = jnp.linspace(0.0, 1.0, RES).astype(x.dtype)
        table = jax.vmap(_fir_fft, in_axes=(0, None))(coeffs, proto).T
        r = jnp.arange(S)
        rel = jnp.abs(r[None, :] - r[:, None]).astype(jnp.float32) / max(S - 1, 1)
        idx = jnp.clip(jnp.round(rel * (RES - 1)).astype(jnp.int32), 0, RES - 1)
        pos_feat = table[idx]
        pos_bias = jnp.einsum('ijf,hf->hij', pos_feat, Wpos)
        qkv = jnp.einsum('bsd,ed->bse', x, Wqkv)
        q, k, v = jnp.split(qkv, 3, axis=-1)
        q = q.reshape(B, S, HEADS, HEAD_DIM)
        k = k.reshape(B, S, HEADS, HEAD_DIM)
        v = v.reshape(B, S, HEADS, HEAD_DIM)
        logits = jnp.einsum('bihd,bjhd->bhij', q, k) * scale + pos_bias[None]
        attn = jax.nn.softmax(logits, axis=-1)
        out = jnp.einsum('bhij,bjhd->bihd', attn, v).reshape(B, S, D)
        return jnp.einsum('bsd,ed->bse', out, Wout)

    def _L0_xattn_ref(x, y, pad_mask, Wq, Wkv):
        import jax, jax.numpy as jnp
        import numpy as np
        NUM_HEADS = 16
        B, N, C = x.shape
        N2 = y.shape[1]
        H = NUM_HEADS
        d = C // H
        scale = d ** (-0.5)
        q = (x @ Wq.T).reshape(B, N, H, d).transpose(0, 2, 1, 3)
        kv = (y @ Wkv.T).reshape(B, N2, 2, H, d).transpose(2, 0, 3, 1, 4)
        k, v = (kv[0], kv[1])
        attn = jnp.einsum('bhnd,bhmd->bhnm', q * scale, k)
        attn = jnp.where(pad_mask[:, None, :, None], attn, jnp.float32(-1000000000.0))
        attn = jax.nn.softmax(attn, axis=-1)
        out = jnp.einsum('bhnm,bhmd->bhnd', attn, v)
        return out.transpose(0, 2, 1, 3).reshape(B, N, C)

    def _L0_ffn_ref(x, Wg, W1, b1, A1, B1, W2, b2, A2, B2, W3, b3, A3, B3):
        import jax, jax.numpy as jnp
        import numpy as np
        DIM = 256
        HID = 512
        E = 8
        K = 2
        R = 16
        B_, S_ = (2, 256)

        def _lora_in(xf, W, b, A, B):
            base = jnp.einsum('td,ehd->teh', xf, W)
            low = jnp.einsum('ter,ehr->teh', jnp.einsum('td,erd->ter', xf, A), B)
            return base + low + b

        def _lora_out(g, W, b, A, B):
            base = jnp.einsum('teh,edh->ted', g, W)
            low = jnp.einsum('ter,edr->ted', jnp.einsum('teh,erh->ter', g, A), B)
            return base + low + b
        orig_shape = x.shape
        xf = x.reshape(-1, x.shape[-1])
        scores = jax.nn.softmax(xf @ Wg.T, axis=-1)
        expert_weights, expert_indices = jax.lax.top_k(scores, K)
        expert_weights = expert_weights / expert_weights.sum(-1, keepdims=True)
        gates = (jax.nn.one_hot(expert_indices, E, dtype=xf.dtype) * expert_weights[..., None]).sum(axis=1)
        h1 = _lora_in(xf, W1, b1, A1, B1)
        h3 = _lora_in(xf, W3, b3, A3, B3)
        g = jax.nn.silu(h1) * h3
        y_e = _lora_out(g, W2, b2, A2, B2)
        y = jnp.einsum('te,ted->td', gates, y_e)
        return y.reshape(orig_shape)
    x = _layernorm(x + _L0_attn_ref(x, L0_attn_Wqkv, L0_attn_Wout, L0_attn_Wpos, L0_attn_coeffs), axis=-1)
    x = _layernorm(x + _L0_xattn_ref(x, ctx_768, mask_BxS_bk0, L0_xattn_Wq, L0_xattn_Wkv), axis=-1)
    x = _layernorm(x + _L0_ffn_ref(x, L0_ffn_Wg, L0_ffn_W1, L0_ffn_b1, L0_ffn_A1, L0_ffn_B1, L0_ffn_W2, L0_ffn_b2, L0_ffn_A2, L0_ffn_B2, L0_ffn_W3, L0_ffn_b3, L0_ffn_A3, L0_ffn_B3), axis=-1)
    return x

_drawn_inputs = setup_inputs


def setup_inputs(seed=0):
    import zlib

    import numpy as np

    out = dict(_drawn_inputs(seed))
    spreads = {'L0_ffn_b1': (0.0, 0.1), 'L0_ffn_b2': (0.0, 0.1), 'L0_ffn_b3': (0.0, 0.1)}
    factors = {'L0_attn_Wpos': 3.149,
     'L0_attn_coeffs': 5.171,
     'L0_ffn_A1': 3.327,
     'L0_ffn_B1': 3.323,
     'L0_ffn_A2': 3.468,
     'L0_ffn_B2': 3.466,
     'L0_ffn_A3': 3.519,
     'L0_ffn_B3': 3.449}
    for name, (base, spread) in spreads.items():
        noise = np.random.default_rng([zlib.crc32(name.encode()), seed]).standard_normal(out[name].shape)
        drawn = base * np.exp(spread * noise) if base else spread * noise
        out[name] = jnp.asarray(drawn.astype(out[name].dtype))
    for name, factor in factors.items():
        out[name] = (out[name] * factor).astype(out[name].dtype)
    return out
```

```python
from contextlib import ExitStack

import numpy as np

import concourse.bass as bass
from concourse import mybir

F32 = mybir.dt.float32
BF16 = mybir.dt.bfloat16
I32 = mybir.dt.int32
U8 = mybir.dt.uint8
ALU = mybir.AluOpType
ACT = mybir.ActivationFunctionType
AXX = mybir.AxisListType.X
RMAX = bass.bass_isa.ReduceOp.max

P = 128
B, S, D = 4, 1024, 256
T = B * S
H, HD = 16, 16
KT = D // P
HG, HPG = 4, 4
SLOTS = 6
ROWS = SLOTS * HD
NORM_ROW = ROWS
CH = 512
NCH = T // CH
JT = S // P
IH = S // CH
STEPS = JT * IH
STRIP = S + (JT - 1) * P
RES, TAPS, NF = 128, 101, 4
Q_PARTS = (0, 0, 0, 1, 1, 2)
K_PARTS = (0, 1, 2, 0, 1, 0)
TINY = 1e-25


def position_tables(nc, io):
    with ExitStack() as ctx:
        def sb(name, shape, dt=F32):
            return ctx.enter_context(nc.sbuf_tensor("pt_" + name, shape, dt))

        def sem(name):
            return ctx.enter_context(nc.semaphore("pt_" + name))

        coeffs = sb("coeffs", [NF, TAPS])
        wpos = sb("wpos", [NF, H])
        ramp = sb("ramp", [TAPS, RES])
        onehot = sb("onehot", [RES, 2 * S])
        combined = sb("combined", [TAPS, H])
        table = sb("table", [RES, H])
        line = sb("line", [H, 2 * S])
        peak = sb("peak", [H, 1])
        ps_small = ctx.enter_context(nc.psum_tensor("pt_small", [P, 2, 512], F32))
        ps_line = ctx.enter_context(nc.psum_tensor("pt_ps_line", [H, 4, 512], F32))
        loaded, mm, copied, stored, strips_stored = (
            sem(n) for n in ("loaded", "mm", "copied", "stored", "strips_stored"))
        block = ctx.enter_context(nc.Block())

        @block.sync
        def _(sp):
            sp.dma_start(coeffs[:, :], io["coeffs"]).then_inc(loaded, 16)
            sp.dma_start(wpos[:, :], io["wposT"]).then_inc(loaded, 16)
            sp.dma_start(ramp[:, :], io["ramp"]).then_inc(loaded, 16)
            sp.dma_start(onehot[:, :], io["onehot"]).then_inc(loaded, 16)
            sp.wait_ge(copied, 4)
            sp.dma_start(io["line"], line[:, :]).then_inc(stored, 16)
            sp.wait_ge(stored, 16)
            for g in range(HG):
                skewed = bass.AP(io["line"].tensor, g * HPG * 2 * S + P - 1, [[2 * S, HPG], [-1, P], [1, STRIP]])
                sp.dma_start(io["strips"][:, g * HPG:(g + 1) * HPG, :].rearrange("p h c -> h p c"),
                             skewed).then_inc(strips_stored, 16)
            sp.wait_ge(strips_stored, 16 * HG)

        @block.tensor
        def _(pe):
            pe.wait_ge(loaded, 64)
            nc.tensor.matmul(ps_small[:TAPS, 0, :H], coeffs[:, :], wpos[:, :], start=True, stop=True).then_inc(mm, 1)
            pe.wait_ge(copied, 1)
            nc.tensor.matmul(ps_small[:RES, 1, :H], ramp[:, :], combined[:, :], start=True, stop=True).then_inc(mm, 1)
            pe.wait_ge(copied, 2)
            for n in range(4):
                last = nc.tensor.matmul(ps_line[:, n, :], table[:, :], onehot[:, n * 512:(n + 1) * 512],
                                        start=True, stop=True)
            last.then_inc(mm, 1)

        @block.vector
        def _(dve):
            dve.wait_ge(mm, 1)
            nc.vector.tensor_copy(combined[:, :], ps_small[:TAPS, 0, :H]).then_inc(copied, 1)
            dve.wait_ge(mm, 2)
            nc.vector.tensor_copy(table[:, :], ps_small[:RES, 1, :H]).then_inc(copied, 1)
            dve.wait_ge(mm, 3)
            flat = ps_line[:, :, :].rearrange("h a b -> h (a b)")
            nc.vector.reduce_max(peak[:, :], flat[:, 0:2 * S - 1], AXX).then_inc(copied, 1)
            dve.wait_ge(copied, 3)
            nc.vector.tensor_scalar(line[:, :], flat, peak[:, 0:1], 4.0, ALU.subtract, ALU.mult).then_inc(copied, 1)


def project_qkv(nc, io):
    with ExitStack() as ctx:
        def sb(name, shape, dt=F32):
            return ctx.enter_context(nc.sbuf_tensor("qp_" + name, shape, dt))

        def sem(name):
            return ctx.enter_context(nc.semaphore("qp_" + name))

        x = [sb(f"x{i}", [P, KT, CH]) for i in range(2)]
        w = sb("w", [P, KT, 3 * D])
        members = sb("members", [P, 8], BF16)
        parts = [sb(f"parts{u}", [P, 3, CH], BF16) for u in range(4)]
        rest = [sb(f"rest{u}", [P, CH]) for u in range(4)]
        squares = [sb(f"squares{u}", [P, CH], BF16) for u in range(4)]
        norms = [sb(f"norms{u}", [8, CH], BF16) for u in range(2)]
        v_out = [sb(f"v_out{i}", [P, 2, H, 32]) for i in range(2)]
        k_peak = sb("k_peak", [P, NCH * 2])
        k_max = sb("k_max", [P, 4])
        ps_u = [ctx.enter_context(nc.psum_tensor(f"qp_ps{u}", [P, CH], F32)) for u in range(6)]
        ps_n = [ctx.enter_context(nc.psum_tensor(f"qp_norm{u}", [8, CH], F32)) for u in range(2)]
        x_loaded = [sem(f"x_loaded{i}") for i in range(2)]
        w_loaded, init_done = sem("w_loaded"), sem("init_done")
        qk_ready, v_ready, norm_ready = sem("qk_ready"), sem("v_ready"), sem("norm_ready")
        hi_done, sq_done, rest_done, mid_done, lo_done = (
            sem(n) for n in ("hi_done", "sq_done", "rest_done", "mid_done", "lo_done"))
        root_done, peak_done, v_copied = sem("root_done"), sem("peak_done"), sem("v_copied")
        unit_stored = [sem(f"unit_stored{u}") for u in range(4)]
        v_stored = [sem(f"v_stored{i}") for i in range(2)]
        kmax_steps = sem("kmax_steps")
        kmax_stored = sem("kmax_stored")
        per_unit = [16 * (SLOTS + 1), 16 * (SLOTS + 1), 16 * SLOTS, 16 * SLOTS]
        block = ctx.enter_context(nc.Block())

        xT = io["xT"].rearrange("(k p) t -> p k t", p=P)

        @block.sync
        def _(sp):
            sp.dma_start(members[:, :], io["members"]).then_inc(w_loaded, 16)
            sp.dma_start(w[:, :, :], io["wqkvT"].rearrange("(k p) e -> p k e", p=P)).then_inc(w_loaded, 16)
            for i in range(2):
                sp.dma_start(x[i][:, :, :], xT[:, :, i * CH:(i + 1) * CH]).then_inc(x_loaded[i], 16)

            def store(c, i):
                for u in range(4):
                    dst = (io["qstack"] if u < 2 else io["kstack"])[u % 2]
                    which = Q_PARTS if u < 2 else K_PARTS
                    for part, ready in ((0, hi_done), (1, mid_done), (2, lo_done)):
                        sp.wait_ge(ready, 4 * c + u + 1)
                        for slot in range(SLOTS):
                            if which[slot] == part:
                                sp.dma_start(dst[slot * P:(slot + 1) * P, bass.ts(c, CH)],
                                             parts[u][:, part, :]).then_inc(unit_stored[u], 16)
                    if u < 2:
                        sp.wait_ge(root_done, 2 * c + u + 1)
                        sp.dma_start(dst[NORM_ROW * 8:NORM_ROW * 8 + 8, bass.ts(c, CH)],
                                     norms[u][:, :]).then_inc(unit_stored[u], 16)
                for n in range(2):
                    sp.wait_ge(v_copied, 2 * c + n + 1)
                    rows = io["vpad"][bass.ds(c * CH + n * 2 * P, 2 * P), :]
                    sp.dma_start(rows.rearrange("(t p) e -> p t e", p=P),
                                 v_out[n][:, :, :, :].rearrange("p t h e -> p t (h e)")).then_inc(v_stored[n], 16)

            with sp.Fori(0, NCH // 2 - 1) as pair:
                for i in range(2):
                    c0 = 2 * pair
                    store(c0 + i, i)
                    sp.dma_start(x[i][:, :, :], xT[:, :, bass.ts(c0 + i + 2, CH)]).then_inc(x_loaded[i], 16)
            for i in range(2):
                store(NCH - 2 + i, i)
            sp.wait_ge(kmax_steps, 5)
            sp.dma_start(io["kmax"], k_max[:, 3:4]).then_inc(kmax_stored, 16)
            sp.wait_ge(kmax_stored, 16)
            for u in range(4):
                sp.wait_ge(unit_stored[u], per_unit[u] * NCH)
            for n in range(2):
                sp.wait_ge(v_stored[n], 16 * NCH)

        @block.tensor
        def _(pe):
            pe.wait_ge(w_loaded, 32)

            def norm(c, u):
                pe.wait_ge(sq_done, 4 * c + u + 1)
                if u < 2:
                    pe.wait_ge(peak_done, 2 * c)
                else:
                    pe.wait_ge(root_done, 2 * c + u - 1)
                nc.tensor.matmul(ps_n[u % 2][:, :], members[:, :], squares[u][:, :],
                                 start=True, stop=True).then_inc(norm_ready, 1)

            with pe.Fori(0, NCH // 2) as pair:
                for i in range(2):
                    c = 2 * pair + i
                    pe.wait_ge(x_loaded[i], 16 * pair + 16)
                    for u in range(4):
                        pe.wait_ge(sq_done, 4 * c)
                        pe.wait_ge(rest_done, 4 * c)
                        for k in range(KT):
                            last = nc.tensor.matmul(ps_u[u][:, :], w[:, k, u * P:(u + 1) * P], x[i][:, k, :],
                                                    start=(k == 0), stop=(k == KT - 1))
                        last.then_inc(qk_ready, 1)
                        if u >= 1:
                            norm(c, u - 1)
                    for n in range(2):
                        pe.wait_ge(v_copied, 2 * c)
                        for t in range(2):
                            for k in range(KT):
                                tok = (2 * n + t) * P
                                last = nc.tensor.matmul(ps_u[4 + n][:, t * D:(t + 1) * D], x[i][:, k, tok:tok + P],
                                                        w[:, k, 2 * D:3 * D], start=(k == 0), stop=(k == KT - 1))
                        last.then_inc(v_ready, 1)
                        if n == 0:
                            norm(c, 3)

        @block.scalar
        def _(act):
            def finish(c, u):
                act.wait_ge(rest_done, 4 * c + u + 1)
                nc.scalar.activation(parts[u][:, 1, :], rest[u][:, :], ACT.Copy).then_inc(mid_done, 1)
                if u < 2:
                    act.wait_ge(norm_ready, 4 * c + u + 1)
                    nc.scalar.activation(norms[u][:, :], ps_n[u % 2][:, :], ACT.Sqrt).then_inc(root_done, 1)

            with act.Fori(0, NCH, 1) as c:
                for u in range(4):
                    act.wait_ge(qk_ready, 4 * c + u + 1)
                    act.wait_ge(unit_stored[u], per_unit[u] * c)
                    nc.scalar.activation(parts[u][:, 0, :], ps_u[u][:, :], ACT.Copy).then_inc(hi_done, 1)
                    nc.scalar.activation(squares[u][:, :], ps_u[u][:, :], ACT.Square).then_inc(sq_done, 1)
                    if u >= 1:
                        finish(c, u - 1)
                finish(c, 3)
            act.wait_ge(kmax_steps, 3)
            nc.scalar.activation(k_max[:, 2:3], k_max[:, 1:2], ACT.Sqrt).then_inc(kmax_steps, 1)

        @block.vector
        def _(dve):
            nc.vector.memset(k_max[:, :], 0.0).then_inc(kmax_steps, 1)
            for n in range(2):
                nc.vector.memset(v_out[n][:, :, :, HD:32], 1.0).then_inc(init_done, 1)
            with dve.Fori(0, NCH, 1) as c:
                for u in range(4):
                    dve.wait_ge(sq_done, 4 * c + u + 1)
                    nc.vector.tensor_tensor(rest[u][:, :], ps_u[u][:, :], parts[u][:, 0, :],
                                            ALU.subtract).then_inc(rest_done, 1)
                for n in range(2):
                    dve.wait_ge(v_ready, 2 * c + n + 1)
                    dve.wait_ge(v_stored[n], 16 * c)
                    nc.vector.tensor_copy(v_out[n][:, :, :, 0:HD],
                                          ps_u[4 + n][:, :].rearrange("p (t h e) -> p t h e", t=2, h=H)
                                          ).then_inc(v_copied, 1)
                for u in range(2):
                    dve.wait_ge(norm_ready, 4 * c + 2 + u + 1)
                    nc.vector.reduce_max(k_peak[0:8, bass.ds(2 * c + u, 1)], ps_n[u][:, :], AXX).then_inc(peak_done, 1)
            dve.wait_ge(peak_done, 2 * NCH)
            nc.vector.reduce_max(k_max[0:8, 0:1], k_peak[0:8, :], AXX).then_inc(kmax_steps, 1)
            dve.wait_ge(kmax_steps, 4)
            nc.vector.tensor_scalar(k_max[:, 3:4], k_max[:, 2:3], -1.05, None, ALU.mult).then_inc(kmax_steps, 1)

        @block.gpsimd
        def _(pool):
            with pool.Fori(0, NCH, 1) as c:
                for u in range(4):
                    pool.wait_ge(mid_done, 4 * c + u + 1)
                    nc.gpsimd.tensor_tensor(parts[u][:, 2, :], rest[u][:, :], parts[u][:, 1, :],
                                            ALU.subtract).then_inc(lo_done, 1)
            pool.wait_ge(kmax_steps, 2)
            nc.gpsimd.partition_all_reduce(k_max[:, 1:2], k_max[:, 0:1], P, RMAX).then_inc(kmax_steps, 1)


def self_attention(nc, io):
    with ExitStack() as ctx:
        def sb(name, shape, dt=F32):
            return ctx.enter_context(nc.sbuf_tensor("sa_" + name, shape, dt))

        def sem(name):
            return ctx.enter_context(nc.semaphore("sa_" + name))

        RING = 4
        strips = sb("strips", [P, HG, HPG, STRIP])
        q = [sb(f"q{i}", [ROWS + 1, HPG, S], BF16) for i in range(2)]
        k = [sb(f"k{i}", [ROWS + 1, HPG, S], BF16) for i in range(2)]
        v = [sb(f"v{i}", [P, JT, P]) for i in range(2)]
        probs = [sb(f"probs{i}", [P, HPG, CH]) for i in range(RING)]
        o_out = [sb(f"o_out{i}", [P, CH]) for i in range(2)]
        k_max = sb("k_max", [P, 1])
        ones = sb("ones", [P, S], BF16)
        zeros = sb("zeros", [P, 4 * D])
        ps_s = [ctx.enter_context(nc.psum_tensor(f"sa_s{i}", [P, 2, CH], F32)) for i in range(2)]
        ps_o = [ctx.enter_context(nc.psum_tensor(f"sa_o{i}", [P, CH], F32)) for i in range(2)]
        strips_loaded, ones_set = sem("strips_loaded"), sem("ones_set")
        zeros_set, table_cleared = sem("zeros_set"), sem("table_cleared")
        kmax_loaded = sem("kmax_loaded")
        shift_set = sem("shift_set")
        loaded = [sem(f"loaded{i}") for i in range(2)]
        scores_ready, added, exp_done, pv_done = (sem(n) for n in ("scores_ready", "added", "exp_done", "pv_done"))
        o_copied = sem("o_copied")
        o_stored = [sem(f"o_stored{i}") for i in range(2)]
        NS = B * STEPS
        block = ctx.enter_context(nc.Block())

        vsrc = io["vpad"].rearrange("(b j p) (g c) -> b g p j c", j=JT, p=P, c=P)

        def rows_of(stack, hg, b, n):
            return bass.AP(stack.tensor, (hg // 2) * ((ROWS + 1) * 8 * T) + (hg % 2) * (4 * T) + b * S,
                           [[8 * T, n], [T, HPG], [1, S]])

        @block.sync
        def _(sp):
            def load(hg, b):
                i = b % 2
                sp.dma_start(q[i][:, :, :], rows_of(io["qstack"], hg, b, ROWS + 1)).then_inc(loaded[i], 16)
                sp.dma_start(k[i][0:ROWS, :, :], rows_of(io["kstack"], hg, b, ROWS)).then_inc(loaded[i], 16)
                sp.dma_start(v[i][:, :, :], vsrc[b, hg]).then_inc(loaded[i], 16)

            def load_strips(hg):
                sp.dma_start(strips[:, hg, :, :], io["strips"][:, bass.ds(hg * HPG, HPG), :]).then_inc(strips_loaded, 16)

            sp.dma_start(k_max[:, :], io["kmax"]).then_inc(kmax_loaded, 16)
            load(0, 0)
            load_strips(0)
            load(0, 1)
            with sp.Fori(0, HG - 1) as hg:
                for b in (2, 3):
                    sp.wait_ge(pv_done, hg * NS + STEPS * (b - 1))
                    load(hg, b)
                load_strips(hg + 1)
                for b in (0, 1):
                    sp.wait_ge(pv_done, hg * NS + STEPS * (b + 3))
                    load(hg + 1, b)
            for b in (2, 3):
                sp.wait_ge(pv_done, (HG - 1) * NS + STEPS * (b - 1))
                load(HG - 1, b)

        @block.tensor
        def _(pe):
            pe.wait_ge(shift_set, 2 * HPG)

            def scores(hg, t):
                b, ih, jt = t // STEPS, (t // JT) % IH, t % JT
                if t % STEPS == 0:
                    pe.wait_ge(loaded[b % 2], 48 * (2 * hg + b // 2) + 48)
                for half in range(2):
                    if t > 0:
                        pe.wait_ge(added, 2 * (hg * NS + t) + half - 1)
                    for n in range(2):
                        h = 2 * half + n
                        last = nc.tensor.matmul(ps_s[half][:, n, :], k[b % 2][:, h, jt * P:(jt + 1) * P],
                                                q[b % 2][:, h, ih * CH:(ih + 1) * CH], start=True, stop=True)
                    last.then_inc(scores_ready, 1)

            def values(hg, t):
                b, ih, jt = t // STEPS, (t // JT) % IH, t % JT
                if jt == 0:
                    pe.wait_ge(o_copied, hg * 2 * B + max(2 * b + ih - 1, 0))
                pe.wait_ge(exp_done, hg * NS + t + 1)
                for h in range(HPG):
                    last = nc.tensor.matmul(ps_o[ih][32 * h:32 * h + 32, :], v[b % 2][:, jt, 32 * h:32 * h + 32],
                                            probs[t % RING][:, h, :], start=(jt == 0), stop=(jt == JT - 1))
                last.then_inc(pv_done, 1)

            LAG = 2
            with pe.Fori(0, HG) as hg:
                for t in range(NS + LAG):
                    if t < NS:
                        scores(hg, t)
                    if t >= LAG:
                        values(hg, t - LAG)

        @block.vector
        def _(dve):
            nc.vector.memset(ones[ROWS:ROWS + 1, :], 1.0).then_inc(ones_set, 1)
            dve.wait_ge(kmax_loaded, 16)
            dve.wait_ge(ones_set, 1)
            for i in range(2):
                for h in range(HPG):
                    nc.vector.tensor_scalar(k[i][ROWS:ROWS + 1, h, :], ones[ROWS:ROWS + 1, :],
                                            k_max[ROWS:ROWS + 1, 0:1], None, ALU.mult).then_inc(shift_set, 1)
            with dve.Fori(0, HG) as hg:
                dve.wait_ge(strips_loaded, 16 * (hg + 1))
                for t in range(NS):
                    ih, jt = (t // JT) % IH, t % JT
                    c0 = ih * CH + (JT - 1 - jt) * P
                    if t >= RING:
                        dve.wait_ge(pv_done, hg * NS + t - RING + 1)
                    else:
                        dve.wait_ge(pv_done, hg * NS)
                    for half in range(2):
                        dve.wait_ge(scores_ready, 2 * (hg * NS + t) + half + 1)
                        nc.vector.tensor_tensor(probs[t % RING][:, 2 * half:2 * half + 2, :], ps_s[half][:, :, :],
                                                strips[:, hg, 2 * half:2 * half + 2, c0:c0 + CH],
                                                ALU.add).then_inc(added, 1)

        @block.scalar
        def _(act):
            def copy_out(hg, n):
                act.wait_ge(pv_done, hg * NS + JT * (n + 1))
                act.wait_ge(o_stored[n % 2], 16 * (hg * B + n // 2))
                nc.scalar.activation(o_out[n % 2][:, :], ps_o[n % 2][:, :], ACT.Copy).then_inc(o_copied, 1)

            with act.Fori(0, HG) as hg:
                for t in range(NS):
                    act.wait_ge(added, 2 * (hg * NS + t) + 2)
                    nc.scalar.activation(probs[t % RING][:, :, :], probs[t % RING][:, :, :], ACT.Exp,
                                         scale=0.25).then_inc(exp_done, 1)
                    if t % JT == 3 and t > JT:
                        copy_out(hg, t // JT - 1)
                copy_out(hg, NS // JT - 1)

        @block.gpsimd
        def _(pool):
            nc.gpsimd.memset(zeros[:, :], 0.0).then_inc(zeros_set, 1)
            pool.wait_ge(zeros_set, 1)
            table = io["table_x"].rearrange("(p n) d -> p (n d)", p=P)
            for n in range(NT // 4):
                pool.dma_start(table[:, n * 4 * D:(n + 1) * 4 * D], zeros[:, :]).then_inc(table_cleared, 16)
            with pool.Fori(0, HG) as hg:
                for n in range(2 * B):
                    pool.wait_ge(o_copied, hg * 2 * B + n + 1)
                    pool.dma_start(io["oT"][hg, :, n * CH:(n + 1) * CH], o_out[n % 2][:, :]).then_inc(o_stored[n % 2], 16)
            for i in range(2):
                pool.wait_ge(o_stored[i], 16 * HG * B)
            pool.wait_ge(table_cleared, 16 * (NT // 4))


def check_and_exact_attention(nc, io):
    with ExitStack() as ctx:
        def sb(name, shape, dt=F32):
            return ctx.enter_context(nc.sbuf_tensor("ex_" + name, shape, dt))

        def sem(name):
            return ctx.enter_context(nc.semaphore("ex_" + name))

        den = sb("den", [P, CH])
        rec = sb("rec", [P, CH])
        low = sb("low", [P, 4])
        flag = sb("flag", [P, 1], I32)
        oT_heads = io["oT"].rearrange("g (h r) t -> (g h) r t", r=32)

        def load_dens(eng, done):
            for n in range(NCH):
                eng.dma_start(den[n * H:(n + 1) * H, :], oT_heads[:, HD, n * CH:(n + 1) * CH]).then_inc(done, 16)

        def store_recs(eng, done):
            for n in range(NCH):
                eng.dma_start(io["rec"][:, n * CH:(n + 1) * CH], rec[n * H:(n + 1) * H, :]).then_inc(done, 16)

        with ExitStack() as inner:
            def sem_a(name):
                return inner.enter_context(nc.semaphore("ck_" + name))

            den_loaded, rec_stored, rec_done, steps = (
                sem_a(n) for n in ("den_loaded", "rec_stored", "rec_done", "steps"))
            block = inner.enter_context(nc.Block())

            @block.sync
            def _(sp):
                load_dens(sp, den_loaded)
                sp.wait_ge(rec_done, 1)
                store_recs(sp, rec_stored)
                sp.wait_ge(rec_stored, 16 * NCH)

            @block.vector
            def _(dve):
                dve.wait_ge(den_loaded, 16 * NCH)
                nc.vector.tensor_reduce(low[:, 0:1], den[:, :], AXX, ALU.min).then_inc(steps, 1)
                dve.wait_ge(steps, 1)
                nc.vector.tensor_scalar(low[:, 1:2], low[:, 0:1], -1.0, None, ALU.mult).then_inc(steps, 1)
                nc.vector.reciprocal(rec[:, :], den[:, :]).then_inc(rec_done, 1)
                dve.wait_ge(steps, 3)
                nc.vector.tensor_scalar(low[:, 3:4], low[:, 2:3], -TINY, 0.0, ALU.is_le, ALU.is_equal).then_inc(steps, 1)
                dve.wait_ge(steps, 4)
                nc.vector.tensor_copy(flag[:, :], low[:, 3:4]).then_inc(steps, 1)

            @block.gpsimd
            def _(pool):
                pool.wait_ge(steps, 2)
                nc.gpsimd.partition_all_reduce(low[:, 2:3], low[:, 1:2], P, RMAX).then_inc(steps, 1)

        SPLIT = 3
        strips = sb("strips", [P, HPG, STRIP])
        q = sb("q", [ROWS + SPLIT, HPG, S], BF16)
        k = sb("k", [ROWS + SPLIT, HPG, S], BF16)
        v = sb("v", [P, JT, P])
        work = sb("work", [P, HPG, CH])
        o_out = sb("o_out", [P, CH])
        ident = sb("ident", [P, P])
        peaks = sb("peaks", [P, HPG * JT])
        shift = sb("shift", [HPG * JT, 2, P])
        shift_parts = sb("shift_parts", [HPG * JT, SPLIT, P], BF16)
        ps_s = [ctx.enter_context(nc.psum_tensor(f"ex_s{i}", [P, 2, CH], F32)) for i in range(2)]
        ps_o = [ctx.enter_context(nc.psum_tensor(f"ex_o{i}", [P, CH], F32)) for i in range(2)]
        ps_t = ctx.enter_context(nc.psum_tensor("ex_t", [HPG * JT, P], F32))
        (ident_loaded, strips_loaded, loaded, ones_set, logits_ready, logits_added, maxed, turned, shift_ready,
         shift_loaded, scores_ready, added, exp_done, pv_done, o_copied, o_stored, den_loaded, rec_done,
         rec_stored) = (sem(n) for n in (
             "ident_loaded", "strips_loaded", "loaded", "ones_set", "logits_ready", "logits_added", "maxed", "turned",
             "shift_ready", "shift_loaded", "scores_ready", "added", "exp_done", "pv_done", "o_copied", "o_stored",
             "den_loaded", "rec_done", "rec_stored"))
        split_steps = sem("split_steps")
        NM = HPG * JT
        block = ctx.enter_context(nc.Block())

        def rows_of(stack, hg, b):
            return bass.AP(stack.tensor, (hg // 2) * ((ROWS + 1) * 8 * T) + (hg % 2) * (4 * T) + b * S,
                           [[8 * T, ROWS], [T, HPG], [1, S]])

        @block.sync
        def _(sp):
            needed = sp.value_load(flag[0:1, 0:1], min_val=0, max_val=1)
            with sp.If(needed > 0):
                sp.dma_start(ident[:, :], io["ident"]).then_inc(ident_loaded, 16)
                with sp.Fori(0, HG) as hg:
                    sp.wait_ge(pv_done, hg * B * STEPS)
                    sp.dma_start(strips[:, :, :], io["strips"][:, bass.ds(hg * HPG, HPG), :]).then_inc(strips_loaded, 16)
                    with sp.Fori(0, B) as b:
                        g = hg * B + b
                        sp.wait_ge(pv_done, g * STEPS)
                        sp.dma_start(q[0:ROWS, :, :], rows_of(io["qstack"], hg, b)).then_inc(loaded, 16)
                        sp.dma_start(k[0:ROWS, :, :], rows_of(io["kstack"], hg, b)).then_inc(loaded, 16)
                        sp.dma_start(v[:, :, :], io["vpad"].rearrange("(b j p) (g c) -> b g p j c", j=JT, p=P, c=P)[b, hg]
                                     ).then_inc(loaded, 16)
                        sp.wait_ge(shift_ready, g + 1)
                        for n in range(SPLIT):
                            sp.dma_start(q[ROWS + n:ROWS + n + 1, :, :].rearrange("p h s -> p (h s)"),
                                         shift_parts[:, n, :]).then_inc(shift_loaded, 16)
                        for ih in range(IH):
                            sp.wait_ge(o_copied, IH * g + ih + 1)
                            sp.dma_start(io["oT"][hg, :, bass.ds(b * S + ih * CH, CH)], o_out[:, :]).then_inc(o_stored, 16)
                sp.wait_ge(o_stored, 16 * IH * HG * B)
                load_dens(sp, den_loaded)
                sp.wait_ge(rec_done, 1)
                store_recs(sp, rec_stored)
                sp.wait_ge(rec_stored, 16 * NCH)

        @block.tensor
        def _(pe):
            needed = pe.value_load(flag[0:1, 0:1], min_val=0, max_val=1)
            with pe.If(needed > 0):
                pe.wait_ge(ident_loaded, 16)
                pe.wait_ge(ones_set, 1)
                with pe.Fori(0, HG * B) as g:
                    pe.wait_ge(loaded, 48 * g + 48)
                    for n in range(NM):
                        h, it = n // JT, n % JT
                        pe.wait_ge(maxed, NM * g + n)
                        if n == 0:
                            pe.wait_ge(added, 2 * STEPS * g)
                        for half in range(2):
                            last = nc.tensor.matmul(ps_s[0][:, half, :], q[0:ROWS, h, it * P:(it + 1) * P],
                                                    k[0:ROWS, h, half * CH:(half + 1) * CH], start=True, stop=True)
                        last.then_inc(logits_ready, 1)
                    pe.wait_ge(maxed, NM * g + NM)
                    nc.tensor.transpose(ps_t[:, :], peaks[:, :], ident[:, :]).then_inc(turned, 1)
                    pe.wait_ge(shift_loaded, 16 * SPLIT * (g + 1))
                    for t in range(STEPS):
                        ih, jt = t // JT, t % JT
                        pe.wait_ge(pv_done, STEPS * g + t)
                        for h in range(HPG):
                            last = nc.tensor.matmul(ps_s[h // 2][:, h % 2, :], k[:, h, jt * P:(jt + 1) * P],
                                                    q[:, h, ih * CH:(ih + 1) * CH], start=True, stop=True)
                            if h % 2:
                                last.then_inc(scores_ready, 1)
                        pe.wait_ge(exp_done, STEPS * g + t + 1)
                        if jt == 0:
                            pe.wait_ge(o_copied, IH * g + ih)
                        for h in range(HPG):
                            last = nc.tensor.matmul(ps_o[ih][32 * h:32 * h + 32, :], v[:, jt, 32 * h:32 * h + 32],
                                                    work[:, h, :], start=(jt == 0), stop=(jt == JT - 1))
                        last.then_inc(pv_done, 1)

        @block.vector
        def _(dve):
            needed = dve.value_load(flag[0:1, 0:1], min_val=0, max_val=1)
            with dve.If(needed > 0):
                nc.vector.memset(k[ROWS:ROWS + SPLIT, :, :], 1.0).then_inc(ones_set, 1)
                with dve.Fori(0, HG) as hg:
                    with dve.Fori(0, B) as b:
                        g = hg * B + b
                        dve.wait_ge(strips_loaded, 16 * hg + 16)
                        for n in range(NM):
                            h, it = n // JT, n % JT
                            dve.wait_ge(logits_ready, NM * g + n + 1)
                            c0 = (JT - 1 - it) * P
                            nc.vector.tensor_tensor(work[:, 0:2, :].rearrange("p a c -> p (a c)"),
                                                    ps_s[0][:, :, :].rearrange("p a c -> p (a c)"),
                                                    strips[:, h, c0:c0 + S], ALU.add).then_inc(logits_added, 1)
                            dve.wait_ge(logits_added, NM * g + n + 1)
                            nc.vector.reduce_max(peaks[:, n:n + 1], work[:, 0:2, :].rearrange("p a c -> p (a c)"),
                                                 AXX).then_inc(maxed, 1)
                        dve.wait_ge(turned, g + 1)
                        nc.vector.tensor_scalar(shift[:, 0, :], ps_t[:, :], -1.0, None, ALU.mult).then_inc(split_steps, 1)
                        dve.wait_ge(split_steps, 5 * g + 1)
                        nc.vector.tensor_copy(shift_parts[:, 0, :], shift[:, 0, :]).then_inc(split_steps, 1)
                        dve.wait_ge(split_steps, 5 * g + 2)
                        nc.vector.tensor_tensor(shift[:, 1, :], shift[:, 0, :], shift_parts[:, 0, :],
                                                ALU.subtract).then_inc(split_steps, 1)
                        dve.wait_ge(split_steps, 5 * g + 3)
                        nc.vector.tensor_copy(shift_parts[:, 1, :], shift[:, 1, :]).then_inc(split_steps, 1)
                        dve.wait_ge(split_steps, 5 * g + 4)
                        nc.vector.tensor_tensor(shift[:, 0, :], shift[:, 1, :], shift_parts[:, 1, :],
                                                ALU.subtract).then_inc(split_steps, 1)
                        dve.wait_ge(split_steps, 5 * g + 5)
                        nc.vector.tensor_copy(shift_parts[:, 2, :], shift[:, 0, :]).then_inc(shift_ready, 1)
                        for t in range(STEPS):
                            ih, jt = t // JT, t % JT
                            c0 = ih * CH + (JT - 1 - jt) * P
                            for half in range(2):
                                dve.wait_ge(scores_ready, 2 * (STEPS * g + t) + half + 1)
                                nc.vector.tensor_tensor(work[:, 2 * half:2 * half + 2, :], ps_s[half][:, :, :],
                                                        strips[:, 2 * half:2 * half + 2, c0:c0 + CH],
                                                        ALU.add).then_inc(added, 1)
                dve.wait_ge(den_loaded, 16 * NCH)
                nc.vector.reciprocal(rec[:, :], den[:, :]).then_inc(rec_done, 1)

        @block.scalar
        def _(act):
            needed = act.value_load(flag[0:1, 0:1], min_val=0, max_val=1)
            with act.If(needed > 0):
                with act.Fori(0, HG * B) as g:
                    for t in range(STEPS):
                        act.wait_ge(added, 2 * (STEPS * g + t) + 2)
                        nc.scalar.activation(work[:, :, :], work[:, :, :], ACT.Exp, scale=0.25).then_inc(exp_done, 1)
                        if t % JT == JT - 1:
                            n = t // JT
                            act.wait_ge(pv_done, STEPS * g + t + 1)
                            act.wait_ge(o_stored, 16 * (IH * g + n))
                            nc.scalar.activation(o_out[:, :], ps_o[n][:, :], ACT.Copy).then_inc(o_copied, 1)


NK, CD = 77, 192
NKB = HPG * NK
TT = CH // P
NTT = T // P
E_, HID, R = 8, 512, 16
EPS = 1e-5


class BankUses:

    def __init__(self, size, keys):
        self.bank = {key: n % size for n, key in enumerate(keys)}
        self.nth = {key: n // size for n, key in enumerate(keys)}
        self.per_pass = [len(range(i, len(keys), size)) for i in range(size)]

    def before(self, it, key):
        return it * self.per_pass[self.bank[key]] + self.nth[key]

    def after(self, it, key):
        return self.before(it, key) + 1


def moments_of(dve, nc, stats_done, stats_count, stats, moments, halves_done, before, done):
    gap = moments[:, :, 2]
    spread = moments[:, :, 3]
    dve.wait_ge(stats_done, stats_count)
    nc.vector.tensor_tensor(gap, stats[:, :, 1], stats[:, :, 4], ALU.subtract).then_inc(halves_done, 1)
    nc.vector.tensor_tensor(moments[:, :, 0:2], stats[:, :, 1:3], stats[:, :, 4:6], ALU.add).then_inc(halves_done, 1)
    dve.wait_ge(halves_done, before + 1)
    nc.vector.scalar_tensor_tensor(out=spread, in0=gap, scalar=0.25, in1=gap, op0=ALU.mult,
                                   op1=ALU.mult).then_inc(halves_done, 1)
    dve.wait_ge(halves_done, before + 3)
    nc.vector.tensor_scalar(moments[:, :, 0], moments[:, :, 0], 0.5, None, ALU.mult).then_inc(halves_done, 1)
    nc.vector.scalar_tensor_tensor(out=moments[:, :, 1], in0=moments[:, :, 1], scalar=1.0 / D, in1=spread,
                                   op0=ALU.mult, op1=ALU.add).then_inc(done, 1)


def cross_block(nc, io, x2_all, logits):
    with ExitStack() as ctx:
        def sb(name, shape, dt=F32):
            return ctx.enter_context(nc.sbuf_tensor("cb_" + name, shape, dt))

        def sem(name):
            return ctx.enter_context(nc.semaphore("cb_" + name))

        wout = sb("wout", [P, KT, D])
        wq = sb("wq", [P, KT, D])
        wg = sb("wg", [P, KT, E_])
        ident = sb("ident", [P, P])
        block8 = sb("block8", [P, 8])
        mask8 = sb("mask8", [P, NTT], U8)
        mask = sb("mask", [P, NTT])
        mask_now = [sb(f"mask_now{i}", [P, TT]) for i in range(2)]
        exponent = sb("exponent", [P, TT])
        eps = sb("eps", [P, TT])
        ctx_a = sb("ctx_a", [P, B * NK])
        ctx_b = sb("ctx_b", [CD - P, B * NK])
        wkv_a = sb("wkv_a", [P, 2 * D])
        wkv_b = sb("wkv_b", [CD - P, 2 * D])
        k_rows = sb("k_rows", [P, KT, B * NK])
        k_diag = sb("k_diag", [P, KT, B, 8 * NK])
        v_all = sb("v_all", [NK, B, H * 32])
        v_now = sb("v_now", [NK, H * 32])
        oc = [sb(f"oc{i}", [P, KT, CH]) for i in range(2)]
        recb = [sb(f"recb{i}", [P, KT, CH]) for i in range(2)]
        x1 = [sb(f"x1{i}", [P, TT, D]) for i in range(2)]
        x1m = [sb(f"x1m{i}", [P, TT, D]) for i in range(2)]
        xT = [sb(f"xT{i}", [P, KT, CH]) for i in range(2)]
        qT = [sb(f"qT{i}", [P, KT, CH]) for i in range(2)]
        peak = [sb(f"peak{i}", [P, H]) for i in range(2)]
        probs = [sb(f"probs{i}", [P, H, NK]) for i in range(2)]
        pT = sb("pT", [NK, H, CH])
        oT = sb("oT", [P, HG, CH])
        dinv = sb("dinv", [P, TT, H])
        stats = [sb(f"stats{i}", [P, TT, 6]) for i in range(2)]
        moments = [sb(f"moments{i}", [P, TT, 4]) for i in range(2)]
        rstd = [sb(f"rstd{i}", [P, TT]) for i in range(2)]
        ps_l = [ctx.enter_context(nc.psum_tensor(f"cb_l{i}", [P, 2, 512], F32)) for i in range(2)]
        ps = [ctx.enter_context(nc.psum_tensor(f"cb_ps{i}", [P, 512], F32)) for i in range(4)]

        keys = []
        for c in range(2):
            keys += [("proj", c, n) for n in range(2)]
        for c in range(2):
            keys += [("x1T", c, k) for k in range(KT)] + [("q", c, k) for k in range(KT)]
        for c in range(2):
            keys += [("pT", c, t, n) for t in range(TT) for n in range(4)]
            keys += [("o", c, g) for g in range(HG)]
            keys += [("o_tok", c, t) for t in range(TT)]
        for c in range(2):
            keys += [("x2T", c, k) for k in range(KT)] + [("gate", c)]
        banks = BankUses(4, keys)
        filled = [sem(f"filled{i}") for i in range(4)]
        drained = [sem(f"drained{i}") for i in range(4)]
        l_filled = [sem(f"l_filled{i}") for i in range(2)]
        l_drained = [sem(f"l_drained{i}") for i in range(2)]

        def wait_drained(eng, it, key):
            eng.wait_ge(drained[banks.bank[key]], banks.after(it, key))

        def wait_filled(eng, it, key):
            eng.wait_ge(filled[banks.bank[key]], banks.after(it, key))

        def drain(instruction, key):
            instruction.then_inc(drained[banks.bank[key]], 1)

        def bank(key):
            return ps[banks.bank[key]]

        w_loaded = sem("w_loaded")
        o_loaded = [sem(f"o_loaded{i}") for i in range(2)]
        x_loaded = [sem(f"x_loaded{i}") for i in range(2)]
        set_up = sem("set_up")
        SET_UP = 1 + KT + 3 + B * (1 + KT)
        setup_mm = sem("setup_mm")
        v_placed, scaled, mask_placed = sem("v_placed"), sem("scaled"), sem("mask_placed")
        summed, stat_done, var_done, rstd_done, normed, masked = (
            sem(n) for n in ("summed", "stat_done", "var_done", "rstd_done", "normed", "masked"))
        peaked, exp_done = sem("peaked"), sem("exp_done")
        inv_done, halves_done = sem("inv_done"), sem("halves_done")
        summed2, stat2_done, var2_done, rstd2_done, normed2 = (
            sem(n) for n in ("summed2", "stat2_done", "var2_done", "rstd2_done", "normed2"))
        block = ctx.enter_context(nc.Block())

        @block.sync
        def _(sp):
            def load(b, c):
                tok = (2 * b + c) * CH
                for k in range(KT):
                    sp.dma_start(oc[c][:, k, :], bass.AP(io["oT"].tensor, tok + k * 2 * P * T,
                                                         [[32 * T, 8], [T, HD], [1, CH]])).then_inc(o_loaded[c], 16)
                    sp.dma_start(recb[c][:, k, :], bass.AP(io["rec"].tensor, tok + k * 8 * T,
                                                           [[T, 8], [0, HD], [1, CH]])).then_inc(o_loaded[c], 16)

            def load_x(b, c):
                sp.dma_start(x1[c][:, :, :], io["x"][bass.ds((2 * b + c) * CH, CH), :].rearrange(
                    "(t p) d -> p t d", p=P)).then_inc(x_loaded[c], 16)

            for dst, name in ((ctx_a, "ctxT_a"), (ctx_b, "ctxT_b"), (wkv_a, "wkvT_a"), (wkv_b, "wkvT_b"),
                              (block8, "block8"), (ident, "ident"), (mask8, "mask")):
                sp.dma_start(dst[:, :], io[name]).then_inc(w_loaded, 16)
            for dst, name in ((wout, "woutT"), (wq, "wqT"), (wg, "wgT")):
                sp.dma_start(dst[:, :, :], io[name].rearrange("(k p) e -> p k e", p=P)).then_inc(w_loaded, 16)
            for c in range(2):
                load(0, c)
                load_x(0, c)
            with sp.Fori(0, B - 1) as b:
                for c in range(2):
                    wait_filled(sp, b, ("proj", c, 1))
                    load(b + 1, c)
                for c in range(2):
                    sp.wait_ge(summed2, TT * (2 * b + c + 1))
                    load_x(b + 1, c)

        @block.tensor
        def _(pe):
            pe.wait_ge(w_loaded, 160)
            for k in range(KT):
                nc.tensor.matmul(ps[k][:, 0:B * NK], wkv_a[:, k * P:(k + 1) * P], ctx_a[:, :], start=True, stop=False)
                nc.tensor.matmul(ps[k][:, 0:B * NK], wkv_b[:, k * P:(k + 1) * P], ctx_b[:, :],
                                 start=False, stop=True).then_inc(setup_mm, 1)
            for b in range(B):
                out = ps_l[b // 2][:NK, b % 2, 0:D]
                nc.tensor.matmul(out, ctx_a[:, b * NK:(b + 1) * NK], wkv_a[:, D:2 * D], start=True, stop=False)
                nc.tensor.matmul(out, ctx_b[:, b * NK:(b + 1) * NK], wkv_b[:, D:2 * D],
                                 start=False, stop=True).then_inc(setup_mm, 1)
            pe.wait_ge(set_up, SET_UP)
            with pe.Fori(0, B) as b:
                def open_bank(key):
                    pe.wait_ge(drained[banks.bank[key]], banks.before(b, key))

                def fill(instruction, key):
                    instruction.then_inc(filled[banks.bank[key]], 1)

                for c in range(2):
                    pe.wait_ge(scaled, 2 * b + c + 1)
                    for n in range(2):
                        open_bank(("proj", c, n))
                        for t in (2 * n, 2 * n + 1):
                            for k in range(KT):
                                last = nc.tensor.matmul(bank(("proj", c, n))[:, t % 2 * D:(t % 2 + 1) * D],
                                                        oc[c][:, k, t * P:(t + 1) * P], wout[:, k, :],
                                                        start=(k == 0), stop=(k == KT - 1))
                        fill(last, ("proj", c, n))
                for c in range(2):
                    for k in range(KT):
                        open_bank(("x1T", c, k))
                        if k == 0:
                            pe.wait_ge(masked, TT * (2 * b + c + 1))
                        for t in range(TT):
                            last = nc.tensor.transpose(bank(("x1T", c, k))[:, t * P:(t + 1) * P],
                                                       x1m[c][:, t, k * P:(k + 1) * P], ident[:, :])
                        fill(last, ("x1T", c, k))
                    for k in range(KT):
                        wait_drained(pe, b, ("x1T", c, k))
                    for m in range(KT):
                        open_bank(("q", c, m))
                        for k in range(KT):
                            last = nc.tensor.matmul(bank(("q", c, m))[:, :], wq[:, k, m * P:(m + 1) * P],
                                                    xT[c][:, k, :], start=(k == 0), stop=(k == KT - 1))
                        fill(last, ("q", c, m))

                def logits_of(c, t):
                    n = 2 * TT * b + TT * c + t
                    for k in range(KT):
                        wait_drained(pe, b, ("q", c, k))
                        pe.wait_ge(l_drained[k], n)
                        for half in range(2):
                            last = nc.tensor.matmul(ps_l[k][:, half, 0:NKB], qT[c][:, k, t * P:(t + 1) * P],
                                                    k_diag[:, k, b, half * NKB:(half + 1) * NKB],
                                                    start=True, stop=True)
                        last.then_inc(l_filled[k], 1)

                def turn_probs(c, t):
                    pe.wait_ge(exp_done, 2 * TT * b + TT * c + t + 1)
                    for n in range(4):
                        open_bank(("pT", c, t, n))
                        for h in range(4):
                            last = nc.tensor.transpose(bank(("pT", c, t, n))[:NK, h * P:(h + 1) * P],
                                                       probs[t % 2][:, 4 * n + h, :], ident[:, :])
                        fill(last, ("pT", c, t, n))

                tiles = [(c, t) for c in range(2) for t in range(TT)]
                logits_of(0, 0)
                for i, (c, t) in enumerate(tiles):
                    if i + 1 < len(tiles):
                        logits_of(*tiles[i + 1])
                    turn_probs(c, t)
                    if t == TT - 1:
                        pe.wait_ge(v_placed, b + 1)
                        for n in range(4):
                            wait_drained(pe, b, ("pT", c, TT - 1, n))
                        for g in range(HG):
                            open_bank(("o", c, g))
                            for h in range(HPG):
                                last = nc.tensor.matmul(bank(("o", c, g))[32 * h:32 * h + 32, :],
                                                        v_now[:, (4 * g + h) * 32:(4 * g + h + 1) * 32],
                                                        pT[:, 4 * g + h, :], start=True, stop=True)
                            fill(last, ("o", c, g))
                        for g in range(HG):
                            wait_drained(pe, b, ("o", c, g))
                        for s in range(TT):
                            open_bank(("o_tok", c, s))
                            for g in range(HG):
                                last = nc.tensor.transpose(bank(("o_tok", c, s))[:, g * P:(g + 1) * P],
                                                           oT[:, g, s * P:(s + 1) * P], ident[:, :])
                            fill(last, ("o_tok", c, s))
                for c in range(2):
                    for k in range(KT):
                        open_bank(("x2T", c, k))
                        if k == 0:
                            pe.wait_ge(normed2, TT * (2 * b + c + 1))
                        for t in range(TT):
                            last = nc.tensor.transpose(bank(("x2T", c, k))[:, t * P:(t + 1) * P],
                                                       x1m[c][:, t, k * P:(k + 1) * P], ident[:, :])
                        fill(last, ("x2T", c, k))
                    for k in range(KT):
                        wait_drained(pe, b, ("x2T", c, k))
                    open_bank(("gate", c))
                    for t in range(TT):
                        for k in range(KT):
                            last = nc.tensor.matmul(bank(("gate", c))[:, t * E_:(t + 1) * E_],
                                                    xT[c][:, k, t * P:(t + 1) * P], wg[:, k, :],
                                                    start=(k == 0), stop=(k == KT - 1))
                    fill(last, ("gate", c))

        @block.scalar
        def _(act):
            with act.Fori(0, B) as b:
                def copy(key, out, scale=1.0, rows=P):
                    wait_filled(act, b, key)
                    src = bank(key)[:rows, :]
                    if key[0] == "pT":
                        src = src.rearrange("p (h t) -> p h t", h=4)
                    drain(nc.scalar.activation(out, src, ACT.Copy, scale=scale), key)

                for c in range(2):
                    for k in range(KT):
                        copy(("x1T", c, k), xT[c][:, k, :])
                    for k in range(KT):
                        copy(("q", c, k), qT[c][:, k, :], scale=HD ** -0.5)

                def exponentials(c, t):
                    n = 2 * TT * b + TT * c + t
                    for k in range(KT):
                        act.wait_ge(l_drained[k], n + 1)
                    nc.scalar.activation(probs[t % 2][:, :, :], probs[t % 2][:, :, :], ACT.Exp).then_inc(exp_done, 1)

                tiles = [(c, t) for c in range(2) for t in range(TT)]
                exponentials(0, 0)
                for i, (c, t) in enumerate(tiles):
                    if i + 1 < len(tiles):
                        exponentials(*tiles[i + 1])
                    for n in range(4):
                        copy(("pT", c, t, n), pT[:, 4 * n:4 * n + 4, t * P:(t + 1) * P], rows=NK)
                    if t == TT - 1:
                        for g in range(HG):
                            copy(("o", c, g), oT[:, g, :])
                for c in range(2):
                    for k in range(KT):
                        copy(("x2T", c, k), xT[c][:, k, :])

        @block.vector
        def _(dve):
            dve.wait_ge(w_loaded, 160)
            nc.vector.tensor_copy(mask[:, :], mask8[:, :]).then_inc(set_up, 1)
            for k in range(KT):
                dve.wait_ge(setup_mm, k + 1)
                nc.vector.tensor_copy(k_rows[:, k, :], ps[k][:, 0:B * NK]).then_inc(set_up, 1)
            nc.vector.memset(v_all[:, :, :], 1.0).then_inc(set_up, 1)
            nc.vector.memset(exponent[:, :], -0.5).then_inc(set_up, 1)
            nc.vector.memset(eps[:, :], EPS).then_inc(set_up, 1)
            dve.wait_ge(set_up, 6)
            for b in range(B):
                dve.wait_ge(setup_mm, KT + b + 1)
                nc.vector.tensor_copy(v_all[:, b, :].rearrange("p (h e) -> p h e", e=32)[:, :, 0:HD],
                                      ps_l[b // 2][:NK, b % 2, 0:D].rearrange("p (h e) -> p h e", e=HD)
                                      ).then_inc(set_up, 1)
                for k in range(KT):
                    nc.vector.tensor_tensor(
                        k_diag[:, k, b, :].rearrange("p (h n) -> p h n", h=8),
                        k_rows[:, k, b * NK:(b + 1) * NK].unsqueeze(1).to_broadcast([P, 8, NK]),
                        block8[:, :].unsqueeze(2).to_broadcast([P, 8, NK]), ALU.mult).then_inc(set_up, 1)

            with dve.Fori(0, B) as b:
                def norm_steps(c, tag, x, done, v_done, r_done, out_done, out_of):
                    n = TT * (2 * b + c)
                    for t in range(TT):
                        nc.vector.bn_stats(stats[c][:, t, :], x[:, t, :]).then_inc(done, 1)
                    moments_of(dve, nc, done, n + TT, stats[c], moments[c], halves_done, 4 * (4 * b + 2 * (tag - 1) + c), v_done)
                    dve.wait_ge(r_done, 2 * (2 * b + c) + 2)
                    for t in range(TT):
                        nc.vector.tensor_scalar(out_of(t), x[:, t, :], moments[c][:, t, 0:1], rstd[c][:, t:t + 1],
                                                ALU.subtract, ALU.mult).then_inc(out_done, 1)

                for c in range(2):
                    dve.wait_ge(x_loaded[c], 16 * b + 16)
                    for n in range(2):
                        key = ("proj", c, n)
                        wait_filled(dve, b, key)
                        drain(nc.vector.tensor_tensor(x1[c][:, 2 * n:2 * n + 2, :],
                                                      bank(key)[:, :].rearrange("p (t d) -> p t d", t=2),
                                                      x1[c][:, 2 * n:2 * n + 2, :], ALU.add), key)
                    for n in range(2):
                        wait_drained(dve, b, ("proj", c, n))
                    norm_steps(c, 1, x1[c], stat_done, var_done, rstd_done, normed, lambda t: x1[c][:, t, :])

                def attend(c):
                    for s in range(TT):
                        key = ("o_tok", c, s)
                        wait_filled(dve, b, key)
                        src = bank(key)[:, :].rearrange("p (h e) -> p h e", e=32)
                        nc.vector.reciprocal(dinv[:, s, :], src[:, :, HD]).then_inc(inv_done, 1)
                        dve.wait_ge(inv_done, TT * (2 * b + c) + s + 1)
                        drain(nc.vector.tensor_tensor(
                            x1m[c][:, s, :].rearrange("p (h e) -> p h e", e=HD), src[:, :, 0:HD],
                            dinv[:, s, :].unsqueeze(2).to_broadcast([P, H, HD]), ALU.mult), key)
                        wait_drained(dve, b, key)
                        nc.vector.tensor_tensor(x1m[c][:, s, :], x1m[c][:, s, :], x1[c][:, s, :],
                                                ALU.add).then_inc(summed2, 1)
                    dve.wait_ge(summed2, TT * (2 * b + c + 1))
                    norm_steps(c, 2, x1m[c], stat2_done, var2_done, rstd2_done, normed2, lambda t: x1m[c][:, t, :])
                tiles = [(c, t) for c in range(2) for t in range(TT)]
                for i, (c, t) in enumerate(tiles):
                    n = 2 * TT * b + i
                    if i >= 2:
                        wait_filled(dve, b, ("pT",) + tiles[i - 2] + (3,))
                    for k in range(KT):
                        src = ps_l[k][:, :, 0:NKB].rearrange("p a (h n) -> p a h n", n=NK)
                        top = peak[t % 2][:, 8 * k:8 * k + 8].rearrange("p (a h) -> p a h", a=2)
                        dve.wait_ge(l_filled[k], n + 1)
                        nc.vector.tensor_reduce(top, src, AXX, ALU.max).then_inc(peaked, 1)
                        dve.wait_ge(peaked, KT * n + k + 1)
                        nc.vector.tensor_tensor(
                            probs[t % 2][:, 8 * k:8 * k + 8, :].rearrange("p (a h) n -> p a h n", a=2), src,
                            top.unsqueeze(3).to_broadcast([P, 2, 4, NK]), ALU.subtract).then_inc(l_drained[k], 1)
                    if i == TT + 1:
                        attend(0)
                attend(1)
                for c in range(2):
                    key = ("gate", c)
                    wait_filled(dve, b, key)
                    drain(nc.vector.tensor_copy(logits[:, bass.ds((2 * b + c) * TT, TT), :],
                                                bank(key)[:, 0:TT * E_].rearrange("p (t e) -> p t e", e=E_)), key)

        @block.gpsimd
        def _(pool):
            pool.wait_ge(set_up, SET_UP)
            with pool.Fori(0, B) as b:
                def roots(c, v_done, r_done):
                    n = 2 * b + c
                    pool.wait_ge(v_done, n + 1)
                    nc.gpsimd.tensor_tensor(rstd[c][:, :], moments[c][:, :, 1], eps[:, :], ALU.add).then_inc(r_done, 1)
                    pool.wait_ge(r_done, 2 * n + 1)
                    nc.gpsimd.tensor_tensor(rstd[c][:, :], rstd[c][:, :], exponent[:, :], ALU.pow).then_inc(r_done, 1)

                for c in range(2):
                    pool.wait_ge(o_loaded[c], 64 * b + 64)
                    nc.gpsimd.tensor_tensor(oc[c][:, :, :], oc[c][:, :, :], recb[c][:, :, :], ALU.mult).then_inc(scaled, 1)
                for c in range(2):
                    roots(c, var_done, rstd_done)
                    nc.gpsimd.tensor_copy(mask_now[c][:, :], mask[:, bass.ds((2 * b + c) * TT, TT)]).then_inc(mask_placed, 1)
                    pool.wait_ge(mask_placed, 2 * b + c + 1)
                    for t in range(TT):
                        pool.wait_ge(normed, TT * (2 * b + c) + t + 1)
                        nc.gpsimd.tensor_tensor(x1m[c][:, t, :], x1[c][:, t, :],
                                                mask_now[c][:, t:t + 1].to_broadcast([P, D]), ALU.mult).then_inc(masked, 1)
                nc.gpsimd.tensor_copy(v_now[:, :], v_all[:, b, :]).then_inc(v_placed, 1)
                for c in range(2):
                    roots(c, var2_done, rstd2_done)
                for c in range(2):
                    for t in range(TT):
                        pool.wait_ge(normed2, TT * (2 * b + c) + t + 1)
                        nc.gpsimd.tensor_copy(x2_all[:, bass.ds((2 * b + c) * TT + t, 1), :], x1m[c][:, t:t + 1, :])


NT = T * 2 // P + E_
FAC = 3 * D + 3 * HID
U32 = mybir.dt.uint32


def route_and_merge(nc, io, x2_all, logits, weights, rows, tile_expert, w1, w3, w2):
    with ExitStack() as ctx:
        def sb(name, shape, dt=F32):
            return ctx.enter_context(nc.sbuf_tensor("ro_" + name, shape, dt))

        def sem(name):
            return ctx.enter_context(nc.semaphore("ro_" + name))

        tri = sb("tri", [P, P])
        ones = sb("ones", [P, P])
        order = sb("order", [P, E_])
        slots = sb("slots", [1, NT])
        factors = [sb(f"factors{i}", [R, FAC]) for i in range(2)]
        first, second, equal, key, rest, total, run, run2 = (
            sb(n, [P, NTT, E_]) for n in ("first", "second", "equal", "key", "rest", "total", "run", "run2"))
        top1, top2, best, e2 = (sb(n, [P, NTT]) for n in ("top1", "top2", "best", "e2"))
        count_i = sb("count_i", [P, 2, E_], I32)
        tiles, ends, ends2 = (sb(n, [P, E_]) for n in ("tiles", "ends", "ends2"))
        place = sb("place", [P, 2, NTT])
        passed = sb("passed", [1, NT, E_])
        owner = sb("owner", [1, NT])
        ps_c = [ctx.enter_context(nc.psum_tensor(f"ro_c{i}", [P, NTT, E_], F32)) for i in range(2)]
        ps_m = [ctx.enter_context(nc.psum_tensor(f"ro_m{i}", [P, HID], F32)) for i in range(6)]
        const_loaded, w_loaded = sem("const_loaded"), sem("w_loaded")
        factors_loaded = [sem(f"factors_loaded{i}") for i in range(2)]
        chosen, counted, exp_done, steps = sem("chosen"), sem("counted"), sem("exp_done"), sem("steps")
        difference, rows_ready, scattered = sem("difference"), sem("rows_ready"), sem("scattered")
        low_rank, merged = sem("low_rank"), sem("merged")
        block = ctx.enter_context(nc.Block())

        @block.sync
        def _(sp):
            for dst, name in ((tri, "tri"), (ones, "all_ones"), (order, "order"), (slots, "slots")):
                sp.dma_start(dst[:, :], io[name]).then_inc(const_loaded, 16)
            for i in range(2):
                sp.dma_start(factors[i][:, :], io["factors"][i]).then_inc(factors_loaded[i], 16)
            for dst, name in ((w1, "w1T"), (w3, "w3T"), (w2, "w2T")):
                sp.dma_start(dst[:, :, :, :], io[name].rearrange("e (k p) n -> p e k n", p=P)).then_inc(w_loaded, 16)
            with sp.Fori(0, E_ // 2 - 1) as pair:
                for i in range(2):
                    sp.wait_ge(low_rank, 6 * (2 * pair + i) + 6)
                    sp.dma_start(factors[i][:, :], io["factors"][2 * pair + i + 2]).then_inc(factors_loaded[i], 16)

        @block.tensor
        def _(pe):
            pe.wait_ge(const_loaded, 64)
            pe.wait_ge(chosen, 1)
            nc.tensor.matmul(ps_c[0][:, :, :], tri[:, :], equal[:, :, :], start=True, stop=True)
            nc.tensor.matmul(ps_c[1][:, :, :], ones[:, :], equal[:, :, :], start=True, stop=True).then_inc(counted, 1)
            with pe.Fori(0, E_ // 2) as pair:
                for i in range(2):
                    pe.wait_ge(factors_loaded[i], 16 * pair + 16)
                    f = factors[i]
                    for n in range(6):
                        pe.wait_ge(merged, 6 * (2 * pair + i))
                        out = ps_m[n]
                        if n < 4:
                            a, b = (n // 2) * D + (n % 2) * P, 3 * D + (n // 2) * HID
                            last = nc.tensor.matmul(out[:, :], f[:, a:a + P], f[:, b:b + HID], start=True, stop=True)
                        else:
                            for m in range(2):
                                a = 3 * D + 2 * HID + (2 * (n - 4) + m) * P
                                last = nc.tensor.matmul(out[:, m * D:(m + 1) * D], f[:, a:a + P],
                                                        f[:, 2 * D:3 * D], start=True, stop=True)
                        last.then_inc(low_rank, 1)

        @block.scalar
        def _(act):
            act.wait_ge(difference, 1)
            nc.scalar.activation(e2[:, :], top2[:, :], ACT.Exp).then_inc(exp_done, 1)

        @block.vector
        def _(dve):
            done = [0]

            def step(instruction):
                done[0] += 1
                instruction.then_inc(steps, 1)
                dve.wait_ge(steps, done[0])

            def over_experts(a):
                return a.unsqueeze(2).to_broadcast([P, NTT, E_])

            def over_tiles(a):
                return a.unsqueeze(1).to_broadcast([P, NTT, E_])

            def pick(values, top, onehot):
                step(nc.vector.tensor_reduce(top, values, AXX, ALU.max))
                step(nc.vector.tensor_tensor(equal[:, :, :], values, over_experts(top), ALU.is_equal))
                step(nc.vector.tensor_tensor(key[:, :, :], equal[:, :, :], over_tiles(order[:, :]), ALU.mult))
                step(nc.vector.tensor_reduce(best[:, :], key[:, :, :], AXX, ALU.max))
                step(nc.vector.tensor_tensor(onehot, key[:, :, :], over_experts(best[:, :]), ALU.is_equal))

            dve.wait_ge(const_loaded, 64)
            pick(logits[:, :, :], top1[:, :], first[:, :, :])
            step(nc.vector.scalar_tensor_tensor(out=rest[:, :, :], in0=first[:, :, :], scalar=-3e38,
                                                in1=logits[:, :, :], op0=ALU.mult, op1=ALU.add))
            pick(rest[:, :, :], top2[:, :], second[:, :, :])
            nc.vector.tensor_tensor(equal[:, :, :], first[:, :, :], second[:, :, :], ALU.add).then_inc(chosen, 1)
            nc.vector.tensor_tensor(top2[:, :], top2[:, :], top1[:, :], ALU.subtract).then_inc(difference, 1)
            dve.wait_ge(exp_done, 1)
            step(nc.vector.tensor_scalar(best[:, :], e2[:, :], 1.0, None, ALU.add))
            step(nc.vector.reciprocal(weights[:, 0, :], best[:, :]))
            step(nc.vector.tensor_tensor(weights[:, 1, :], e2[:, :], weights[:, 0, :], ALU.mult))
            dve.wait_ge(counted, 1)
            step(nc.vector.tensor_copy(total[:, :, :], ps_c[1][:, :, :]))
            src, dst = total, run
            for shift in (1, 2, 4, 8, 16):
                nc.vector.tensor_copy(dst[:, 0:shift, :], src[:, 0:shift, :])
                step(nc.vector.tensor_tensor(dst[:, shift:, :], src[:, shift:, :], src[:, :NTT - shift, :], ALU.add))
                src, dst = dst, (run2 if dst is run else run)
            step(nc.vector.tensor_scalar(count_i[:, 0, :], src[:, NTT - 1, :], float(P - 1), None, ALU.add))
            step(nc.vector.tensor_scalar(count_i[:, 1, :], count_i[:, 0, :], 7, None, ALU.arith_shift_right))
            step(nc.vector.tensor_copy(tiles[:, :], count_i[:, 1, :]))
            a, b = tiles, ends
            for shift in (1, 2, 4):
                nc.vector.tensor_copy(b[:, 0:shift], a[:, 0:shift])
                step(nc.vector.tensor_tensor(b[:, shift:], a[:, shift:], a[:, :E_ - shift], ALU.add))
                a, b = b, (ends2 if b is ends else ends)
            last_tile = a
            step(nc.vector.tensor_tensor(b[:, :], last_tile[:, :], tiles[:, :], ALU.subtract))
            step(nc.vector.tensor_scalar(b[:, :], b[:, :], float(P), None, ALU.mult))
            step(nc.vector.tensor_tensor(key[:, :, :], src[:, :, :], total[:, :, :], ALU.subtract))
            step(nc.vector.tensor_tensor(key[:, :, :], ps_c[0][:, :, :], key[:, :, :], ALU.add))
            step(nc.vector.tensor_tensor(key[:, :, :], key[:, :, :], over_tiles(b[:, :]), ALU.add))
            for n, onehot in enumerate((first, second)):
                step(nc.vector.tensor_tensor(rest[:, :, :], key[:, :, :], onehot[:, :, :], ALU.mult))
                step(nc.vector.tensor_reduce(place[:, n, :], rest[:, :, :], AXX, ALU.add))
            nc.vector.tensor_copy(rows[:, :, :], place[:, :, :]).then_inc(rows_ready, 1)
            step(nc.vector.tensor_tensor(passed[:, :, :], slots[:, :].unsqueeze(2).to_broadcast([1, NT, E_]),
                                         last_tile[0:1, :].unsqueeze(1).to_broadcast([1, NT, E_]), ALU.is_ge))
            step(nc.vector.tensor_reduce(owner[:, :], passed[:, :, :], AXX, ALU.add))
            step(nc.vector.tensor_scalar(owner[:, :], owner[:, :], float(E_ - 1), None, ALU.min))
            step(nc.vector.tensor_copy(tile_expert[:, :], owner[:, :]))

            dve.wait_ge(w_loaded, 48)
            with dve.Fori(0, E_) as e:
                for n in range(6):
                    target = (w1, w3, w2)[n // 2]
                    if n < 4:
                        into = target[:, e, n % 2, :]
                    else:
                        into = target[:, e, 2 * (n - 4):2 * (n - 4) + 2, :].rearrange("p a d -> p (a d)")
                    dve.wait_ge(low_rank, 6 * e + n + 1)
                    nc.vector.tensor_tensor(into, ps_m[n][:, :], into, ALU.add).then_inc(merged, 1)

        @block.gpsimd
        def _(pool):
            pool.wait_ge(rows_ready, 1)
            for t in range(NTT):
                for n in range(2):
                    pool.indirect_dma_start(out=io["table_x"], out_offset=bass.IndirectOffsetOnAxis(rows[:, n, t:t + 1], 0),
                                            in_=x2_all[:, t, :], in_offset=None).then_inc(scattered, 16)
            pool.wait_ge(scattered, 16 * 2 * NTT)


def experts(nc, io, tile_expert, w1, w3, w2):
    with ExitStack() as ctx:
        def sb(name, shape, dt=F32):
            return ctx.enter_context(nc.sbuf_tensor("xp_" + name, shape, dt))

        def sem(name):
            return ctx.enter_context(nc.semaphore("xp_" + name))

        KH = HID // P
        b13 = sb("b13", [P, E_, 2, HID])
        b2 = sb("b2", [P, E_, D])
        ident = sb("ident", [P, P])
        x = [sb(f"x{i}", [P, D]) for i in range(2)]
        xT = [sb(f"xT{i}", [P, KT, P]) for i in range(2)]
        h = [sb(f"h{i}", [P, 2, HID]) for i in range(2)]
        g = [sb(f"g{i}", [P, HID]) for i in range(2)]
        gT = [sb(f"gT{i}", [P, KH, P]) for i in range(2)]
        y = [sb(f"y{i}", [P, D]) for i in range(2)]
        ps_h = [ctx.enter_context(nc.psum_tensor(f"xp_ps_h{i}", [P, 2, HID], F32)) for i in range(2)]
        ps_x = ctx.enter_context(nc.psum_tensor("xp_ps_x", [P, KT, P], F32))
        ps_g = ctx.enter_context(nc.psum_tensor("xp_ps_g", [P, KH, P], F32))
        ps_y = ctx.enter_context(nc.psum_tensor("xp_ps_y", [P, 512], F32))
        const_loaded = sem("const_loaded")
        x_loaded = [sem(f"x_loaded{i}") for i in range(2)]
        y_stored = [sem(f"y_stored{i}") for i in range(2)]
        (x_turned, x_copied, h_ready, biased, silu_done, g_done, g_turned, g_copied, y_ready, y_done) = (
            sem(n) for n in ("x_turned", "x_copied", "h_ready", "biased", "silu_done", "g_done", "g_turned",
                             "g_copied", "y_ready", "y_done"))
        block = ctx.enter_context(nc.Block())

        LOOPED = NT - 4

        def pipeline(eng, head, body, tail):
            head()
            with eng.Fori(0, LOOPED // 2) as pair:
                for i in range(2):
                    body(2 * pair + 1 + i, 1 + i)
            tail()

        @block.sync
        def _(sp):
            sp.dma_start(ident[:, :], io["ident"]).then_inc(const_loaded, 16)

            def load(s, parity):
                sp.dma_start(x[parity % 2][:, :], io["table_x"][bass.ds(s * P, P), :]).then_inc(x_loaded[parity % 2], 16)

            load(0, 0)
            load(1, 1)
            sp.dma_start(b13[:, :, :, :].rearrange("p e a h -> p (e a h)"),
                         bass.AP(io["b13"].tensor, 0, [[0, P], [1, E_ * 2 * HID]])).then_inc(const_loaded, 16)
            sp.dma_start(b2[:, :, :].rearrange("p e d -> p (e d)"),
                         bass.AP(io["b2"].tensor, 0, [[0, P], [1, E_ * D]])).then_inc(const_loaded, 16)

            def store(s, parity):
                sp.wait_ge(y_done, s + 1)
                sp.dma_start(io["table_y"][bass.ds(s * P, P), :], y[parity % 2][:, :]).then_inc(y_stored[parity % 2], 16)

            def next_x(s, parity):
                sp.wait_ge(x_turned, s - 1)
                load(s, parity)

            next_x(2, 0)
            next_x(3, 1)
            with sp.Fori(0, (NT - 4) // 2) as pair:
                for i in range(2):
                    next_x(2 * pair + 4 + i, i)
                    store(2 * pair + i, i)
            for s in range(NT - 4, NT):
                store(s, s)
            for i in range(2):
                sp.wait_ge(y_stored[i], 16 * NT // 2)

        @block.tensor
        def _(pe):
            pe.wait_ge(const_loaded, 48)

            def turn_x(s, parity, pair):
                pe.wait_ge(x_loaded[parity % 2], 16 * pair + 16)
                pe.wait_ge(x_copied, s)
                for k in range(KT):
                    last = nc.tensor.transpose(ps_x[:, k, :], x[parity % 2][:, k * P:(k + 1) * P], ident[:, :])
                last.then_inc(x_turned, 1)

            def hidden(s, parity):
                e = pe.value_load(tile_expert[0:1, bass.ds(s, 1)], min_val=0, max_val=E_ - 1)
                pe.wait_ge(x_copied, s + 1)
                for n, w in enumerate((w1, w3)):
                    for k in range(KT):
                        last = nc.tensor.matmul(ps_h[parity % 2][:, n, :], xT[parity % 2][:, k, :], w[:, e, k, :],
                                                start=(k == 0), stop=(k == KT - 1))
                last.then_inc(h_ready, 1)

            def turn_g(s, parity):
                pe.wait_ge(g_done, s + 1)
                pe.wait_ge(g_copied, s)
                for k in range(KH):
                    last = nc.tensor.transpose(ps_g[:, k, :], g[parity % 2][:, k * P:(k + 1) * P], ident[:, :])
                last.then_inc(g_turned, 1)

            def out(s, parity):
                e = pe.value_load(tile_expert[0:1, bass.ds(s, 1)], min_val=0, max_val=E_ - 1)
                pe.wait_ge(g_copied, s + 1)
                pe.wait_ge(y_done, s)
                for k in range(KH):
                    last = nc.tensor.matmul(ps_y[:, 0:D], gT[parity % 2][:, k, :], w2[:, e, k, :],
                                            start=(k == 0), stop=(k == KH - 1))
                last.then_inc(y_ready, 1)

            def head():
                turn_x(0, 0, 0)
                hidden(0, 0)
                turn_x(1, 1, 0)
                hidden(1, 1)
                turn_x(2, 0, 1)
                turn_g(0, 0)

            def body(s, parity):
                hidden(s + 1, parity + 1)
                turn_x(s + 2, parity, pair_of(s, parity))
                turn_g(s, parity)
                out(s - 1, parity - 1)

            def pair_of(s, parity):
                return s // 2 + 1

            def tail():
                for s in range(NT - 3, NT):
                    if s + 1 < NT:
                        hidden(s + 1, s + 1)
                    if s + 2 < NT:
                        turn_x(s + 2, s, (s + 2) // 2)
                    turn_g(s, s)
                    out(s - 1, s - 1)
                out(NT - 1, NT - 1)

            pipeline(pe, head, body, tail)

        @block.scalar
        def _(act):
            def copy_x(s, parity):
                act.wait_ge(x_turned, s + 1)
                nc.scalar.activation(xT[parity % 2][:, :, :], ps_x[:, :, :], ACT.Copy).then_inc(x_copied, 1)

            def copy_g(s, parity):
                act.wait_ge(g_turned, s + 1)
                nc.scalar.activation(gT[parity % 2][:, :, :], ps_g[:, :, :], ACT.Copy).then_inc(g_copied, 1)

            def silu(s, parity):
                act.wait_ge(biased, s + 1)
                nc.scalar.activation(h[parity % 2][:, 0, :], h[parity % 2][:, 0, :], ACT.Silu).then_inc(silu_done, 1)

            def head():
                copy_x(0, 0)
                copy_x(1, 1)
                silu(0, 0)
                copy_x(2, 0)
                copy_g(0, 0)
                silu(1, 1)

            def body(s, parity):
                copy_x(s + 2, parity)
                copy_g(s, parity)
                silu(s + 1, parity + 1)

            def tail():
                for s in range(NT - 3, NT):
                    if s + 2 < NT:
                        copy_x(s + 2, s)
                    copy_g(s, s)
                    if s + 1 < NT:
                        silu(s + 1, s + 1)

            pipeline(act, head, body, tail)

        @block.vector
        def _(dve):
            dve.wait_ge(const_loaded, 48)

            def gate(s, parity):
                i = parity % 2
                e = dve.value_load(tile_expert[0:1, bass.ds(s, 1)], min_val=0, max_val=E_ - 1)
                dve.wait_ge(h_ready, s + 1)
                nc.vector.tensor_tensor(h[i][:, :, :], ps_h[i][:, :, :], b13[:, e, :, :], ALU.add).then_inc(biased, 1)
                dve.wait_ge(silu_done, s + 1)
                nc.vector.tensor_tensor(g[i][:, :], h[i][:, 0, :], h[i][:, 1, :], ALU.mult).then_inc(g_done, 1)

            def out(s, parity):
                i = parity % 2
                e = dve.value_load(tile_expert[0:1, bass.ds(s, 1)], min_val=0, max_val=E_ - 1)
                dve.wait_ge(y_ready, s + 1)
                dve.wait_ge(y_stored[i], stored_before(s, parity))
                nc.vector.tensor_tensor(y[i][:, :], ps_y[:, 0:D], b2[:, e, :], ALU.add).then_inc(y_done, 1)

            def stored_before(s, parity):
                return 16 * (s // 2)

            def head():
                gate(0, 0)
                gate(1, 1)

            def body(s, parity):
                gate(s + 1, parity + 1)
                out(s - 1, parity - 1)

            def tail():
                for s in range(NT - 3, NT):
                    if s + 1 < NT:
                        gate(s + 1, s + 1)
                    out(s - 1, s - 1)
                out(NT - 1, NT - 1)

            pipeline(dve, head, body, tail)


def combine(nc, io, x2_all, weights, rows):
    with ExitStack() as ctx:
        def sb(name, shape, dt=F32):
            return ctx.enter_context(nc.sbuf_tensor("co_" + name, shape, dt))

        def sem(name):
            return ctx.enter_context(nc.semaphore("co_" + name))

        ya = [sb(f"ya{i}", [P, TT, D]) for i in range(2)]
        yb = [sb(f"yb{i}", [P, TT, D]) for i in range(2)]
        out = [sb(f"out{i}", [P, TT, D]) for i in range(2)]
        stats = [sb(f"stats{i}", [P, TT, 6]) for i in range(2)]
        moments = [sb(f"moments{i}", [P, TT, 4]) for i in range(2)]
        rstd = [sb(f"rstd{i}", [P, TT]) for i in range(2)]
        exponent = sb("exponent", [P, TT])
        eps = sb("eps", [P, TT])
        gathered = [sem(f"gathered{i}") for i in range(2)]
        exponent_set, halves_done, partial, summed, stat_done, var_done, rstd_done, normed = (
            sem(n) for n in ("exponent_set", "halves_done", "partial", "summed", "stat_done", "var_done", "rstd_done", "normed"))
        stored = [sem(f"stored{i}") for i in range(2)]
        block = ctx.enter_context(nc.Block())

        @block.gpsimd
        def _(pool):
            def gather(c):
                if c >= 2:
                    pool.wait_ge(summed, TT * (c - 1))
                for t in range(TT):
                    for n, dst in enumerate((ya, yb)):
                        pool.indirect_dma_start(
                            out=dst[c % 2][:, t, :], out_offset=None, in_=io["table_y"],
                            in_offset=bass.IndirectOffsetOnAxis(rows[:, n, c * TT + t:c * TT + t + 1], 0)
                        ).then_inc(gathered[c % 2], 16)

            gather(0)
            for c in range(NCH):
                if c + 1 < NCH:
                    gather(c + 1)
                pool.wait_ge(var_done, c + 1)
                nc.gpsimd.tensor_tensor(rstd[c % 2][:, :], moments[c % 2][:, :, 1], eps[:, :], ALU.add).then_inc(rstd_done, 1)
                if c == 0:
                    pool.wait_ge(exponent_set, 2)
                pool.wait_ge(rstd_done, 2 * c + 1)
                nc.gpsimd.tensor_tensor(rstd[c % 2][:, :], rstd[c % 2][:, :], exponent[:, :], ALU.pow).then_inc(rstd_done, 1)

        @block.vector
        def _(dve):
            nc.vector.memset(exponent[:, :], -0.5).then_inc(exponent_set, 1)
            nc.vector.memset(eps[:, :], EPS).then_inc(exponent_set, 1)

            def add_up(pair, i):
                c = 2 * pair + i
                dve.wait_ge(gathered[i], 16 * 2 * TT * (pair + 1))
                for t in range(TT):
                    n = c * TT + t
                    nc.vector.scalar_tensor_tensor(out=ya[i][:, t, :], in0=ya[i][:, t, :],
                                                   scalar=weights[:, 0, bass.ds(n, 1)], in1=x2_all[:, n, :],
                                                   op0=ALU.mult, op1=ALU.add).then_inc(partial, 1)
                for t in range(TT):
                    n = c * TT + t
                    dve.wait_ge(partial, n + 1)
                    if t == 0:
                        dve.wait_ge(stored[i], 16 * pair)
                    nc.vector.scalar_tensor_tensor(out=out[i][:, t, :], in0=yb[i][:, t, :],
                                                   scalar=weights[:, 1, bass.ds(n, 1)], in1=ya[i][:, t, :],
                                                   op0=ALU.mult, op1=ALU.add).then_inc(summed, 1)
                for t in range(TT):
                    dve.wait_ge(summed, c * TT + t + 1)
                    nc.vector.bn_stats(stats[i][:, t, :], out[i][:, t, :]).then_inc(stat_done, 1)
                moments_of(dve, nc, stat_done, c * TT + TT, stats[i], moments[i], halves_done, 4 * c, var_done)

            def normalise(pair, i):
                c = 2 * pair + i
                dve.wait_ge(rstd_done, 2 * c + 2)
                for t in range(TT):
                    nc.vector.tensor_scalar(out[i][:, t, :], out[i][:, t, :], moments[i][:, t, 0:1],
                                            rstd[i][:, t:t + 1], ALU.subtract, ALU.mult).then_inc(normed, 1)

            with dve.Fori(0, NCH // 2) as pair:
                for i in range(2):
                    add_up(pair, i)
                    normalise(pair, i)

        @block.sync
        def _(sp):
            with sp.Fori(0, NCH // 2) as pair:
                for i in range(2):
                    c = 2 * pair + i
                    sp.wait_ge(normed, TT * (c + 1))
                    sp.dma_start(io["out"][bass.ds(c * CH, CH), :].rearrange("(t p) d -> p t d", p=P),
                                 out[i][:, :, :]).then_inc(stored[i], 16)
            for i in range(2):
                sp.wait_ge(stored[i], 16 * NCH // 2)


def decoder_layer(nc, io):
    def scratch(name, shape, dt=F32):
        io[name] = nc.dram_tensor(name, shape, dt).ap()

    scratch("line", [H, 2 * S])
    scratch("strips", [P, H, STRIP])
    scratch("qstack", [2, (ROWS + 1) * 8, T], BF16)
    scratch("kstack", [2, (ROWS + 1) * 8, T], BF16)
    scratch("vpad", [T, H * 32])
    scratch("kmax", [P, 1])
    scratch("oT", [HG, P, T])
    scratch("rec", [H, T])
    scratch("table_x", [NT * P, D])
    scratch("table_y", [NT * P, D])
    io["out"] = io["out"].rearrange("b s d -> (b s) d")
    position_tables(nc, io)
    project_qkv(nc, io)
    self_attention(nc, io)
    check_and_exact_attention(nc, io)
    with ExitStack() as ctx:
        def sb(name, shape, dt=F32):
            return ctx.enter_context(nc.sbuf_tensor(name, shape, dt))

        x2_all = sb("x2_all", [P, NTT, D])
        logits = sb("logits", [P, NTT, E_])
        cross_block(nc, io, x2_all, logits)
        weights = sb("weights", [P, 2, NTT])
        rows = sb("rows", [P, 2, NTT], U32)
        tile_expert = sb("tile_expert", [1, NT], I32)
        with ExitStack() as inner:
            w1 = inner.enter_context(nc.sbuf_tensor("w1", [P, E_, KT, HID], F32))
            w3 = inner.enter_context(nc.sbuf_tensor("w3", [P, E_, KT, HID], F32))
            w2 = inner.enter_context(nc.sbuf_tensor("w2", [P, E_, HID // P, D], F32))
            route_and_merge(nc, io, x2_all, logits, weights, rows, tile_expert, w1, w3, w2)
            experts(nc, io, tile_expert, w1, w3, w2)
        combine(nc, io, x2_all, weights, rows)


def constants():
    dist = np.abs(np.arange(2 * S) - (S - 1)).astype(np.float32)
    index = np.clip(np.round(dist / np.float32(S - 1) * np.float32(RES - 1)).astype(np.int32), 0, RES - 1)
    proto = np.linspace(0.0, 1.0, RES).astype(np.float32)
    ramp = np.zeros((TAPS, RES), np.float32)
    for tap in range(TAPS):
        ramp[tap, tap:] = proto[:RES - tap]
    p = np.arange(P)
    return {
        "onehot": (np.arange(RES)[:, None] == index[None, :]).astype(np.float32),
        "ramp": ramp,
        "ident": np.eye(P, dtype=np.float32),
        "block8": (p[:, None] // HD == np.arange(8)[None, :]).astype(np.float32),
        "members": (p[:, None] % 8 == np.arange(8)[None, :]).astype(mybir.dt.np(BF16)),
        "tri": (p[:, None] < p[None, :]).astype(np.float32),
        "all_ones": np.ones((P, P), np.float32),
        "order": np.tile(np.arange(E_, 0, -1, dtype=np.float32), (P, 1)),
        "slots": np.arange(NT, dtype=np.float32)[None, :],
    }


def laid_out(x, ctx_768, mask_BxS_bk0, L0_attn_Wqkv, L0_attn_Wout, L0_attn_Wpos, L0_attn_coeffs, L0_xattn_Wq,
             L0_xattn_Wkv, L0_ffn_Wg, L0_ffn_W1, L0_ffn_b1, L0_ffn_A1, L0_ffn_B1, L0_ffn_W2, L0_ffn_b2, L0_ffn_A2,
             L0_ffn_B2, L0_ffn_W3, L0_ffn_b3, L0_ffn_A3, L0_ffn_B3):
    def turned(w):
        return w.transpose(0, 2, 1)

    by_dim = np.arange(D).reshape(2, 8, HD).transpose(0, 2, 1).ravel()
    order = np.concatenate([by_dim, D + by_dim, 2 * D + np.arange(D)])
    xf = x.reshape(T, D)
    ctxT = ctx_768.reshape(B * NK, CD).T
    wkvT = L0_xattn_Wkv.T
    return {
        "x": xf, "xT": xf.T,
        "wqkvT": L0_attn_Wqkv[order].T, "coeffs": L0_attn_coeffs, "wposT": L0_attn_Wpos.T,
        "woutT": L0_attn_Wout.T, "wqT": L0_xattn_Wq.T, "wgT": L0_ffn_Wg.T,
        "ctxT_a": ctxT[:P], "ctxT_b": ctxT[P:], "wkvT_a": wkvT[:P], "wkvT_b": wkvT[P:],
        "mask": mask_BxS_bk0.reshape(NTT, P).T,
        "w1T": turned(L0_ffn_W1), "w3T": turned(L0_ffn_W3), "w2T": turned(L0_ffn_W2),
        "factors": np.concatenate([L0_ffn_A1, L0_ffn_A3, turned(L0_ffn_B2), turned(L0_ffn_B1), turned(L0_ffn_B3),
                                   L0_ffn_A2], axis=2),
        "b13": np.stack([L0_ffn_b1, L0_ffn_b3], axis=1), "b2": L0_ffn_b2,
    }


def kernel(**inputs):
    import concourse.bacc as bacc
    from concourse.bass_utils import run_bass_kernel_spmd

    nc = bacc.Bacc("TRN2", target_bir_lowering=False, num_devices=1)
    arrays, io = {}, {}
    for name, a in {**laid_out(**{k: np.asarray(v) for k, v in inputs.items()}), **constants()}.items():
        arrays[name] = np.ascontiguousarray(a)
        io[name] = nc.dram_tensor(name, a.shape, mybir.dt.from_np(a.dtype), kind="ExternalInput").ap()
    io["out"] = nc.dram_tensor("out", (B, S, D), F32, kind="ExternalOutput").ap()
    decoder_layer(nc, io)
    return run_bass_kernel_spmd(nc, [arrays], core_ids=[0]).results[0]["out"]
```

```python
from contextlib import ExitStack

import numpy as np

import concourse.bass as bass
from concourse import mybir

F32 = mybir.dt.float32
BF16 = mybir.dt.bfloat16
I32 = mybir.dt.int32
U8 = mybir.dt.uint8
ALU = mybir.AluOpType
ACT = mybir.ActivationFunctionType
AXX = mybir.AxisListType.X
RMAX = bass.bass_isa.ReduceOp.max

P = 128
B, S, D = 4, 1024, 256
T = B * S
H, HD = 16, 16
KT = D // P
HG, HPG = 4, 4
SLOTS = 6
ROWS = SLOTS * HD
NORM_ROW = ROWS
CH = 512
NCH = T // CH
JT = S // P
IH = S // CH
STEPS = JT * IH
STRIP = S + (JT - 1) * P
RES, TAPS, NF = 128, 101, 4
Q_PARTS = (0, 0, 0, 1, 1, 2)
K_PARTS = (0, 1, 2, 0, 1, 0)
TINY = 1e-25


def position_tables(nc, io):
    with ExitStack() as ctx:
        def sb(name, shape, dt=F32):
            return ctx.enter_context(nc.sbuf_tensor("pt_" + name, shape, dt))

        def sem(name):
            return ctx.enter_context(nc.semaphore("pt_" + name))

        coeffs = sb("coeffs", [NF, TAPS])
        wpos = sb("wpos", [NF, H])
        ramp = sb("ramp", [TAPS, RES])
        onehot = sb("onehot", [RES, 2 * S])
        combined = sb("combined", [TAPS, H])
        table = sb("table", [RES, H])
        line = sb("line", [H, 2 * S])
        peak = sb("peak", [H, 1])
        ps_small = ctx.enter_context(nc.psum_tensor("pt_small", [P, 2, 512], F32))
        ps_line = ctx.enter_context(nc.psum_tensor("pt_ps_line", [H, 4, 512], F32))
        loaded, mm, copied, stored = (sem(n) for n in ("loaded", "mm", "copied", "stored"))
        block = ctx.enter_context(nc.Block())

        @block.sync
        def _(sp):
            sp.dma_start(coeffs[:, :], io["coeffs"]).then_inc(loaded, 16)
            sp.dma_start(wpos[:, :], io["wposT"]).then_inc(loaded, 16)
            sp.dma_start(ramp[:, :], io["ramp"]).then_inc(loaded, 16)
            sp.dma_start(onehot[:, :], io["onehot"]).then_inc(loaded, 16)
            sp.wait_ge(copied, 4)
            sp.dma_start(io["line"], line[:, :]).then_inc(stored, 16)
            sp.wait_ge(stored, 16)

        @block.tensor
        def _(pe):
            pe.wait_ge(loaded, 64)
            nc.tensor.matmul(ps_small[:TAPS, 0, :H], coeffs[:, :], wpos[:, :], start=True, stop=True).then_inc(mm, 1)
            pe.wait_ge(copied, 1)
            nc.tensor.matmul(ps_small[:RES, 1, :H], ramp[:, :], combined[:, :], start=True, stop=True).then_inc(mm, 1)
            pe.wait_ge(copied, 2)
            for n in range(4):
                last = nc.tensor.matmul(ps_line[:, n, :], table[:, :], onehot[:, n * 512:(n + 1) * 512],
                                        start=True, stop=True)
            last.then_inc(mm, 1)

        @block.vector
        def _(dve):
            dve.wait_ge(mm, 1)
            nc.vector.tensor_copy(combined[:, :], ps_small[:TAPS, 0, :H]).then_inc(copied, 1)
            dve.wait_ge(mm, 2)
            nc.vector.tensor_copy(table[:, :], ps_small[:RES, 1, :H]).then_inc(copied, 1)
            dve.wait_ge(mm, 3)
            flat = ps_line[:, :, :].rearrange("h a b -> h (a b)")
            nc.vector.reduce_max(peak[:, :], flat[:, 0:2 * S - 1], AXX).then_inc(copied, 1)
            dve.wait_ge(copied, 3)
            nc.vector.tensor_scalar(line[:, :], flat, peak[:, 0:1], 4.0, ALU.subtract, ALU.mult).then_inc(copied, 1)


def skew(eng, io, hg):
    lines = bass.AP(io["line"].tensor, hg * HPG * 2 * S + P - 1, [[2 * S, HPG], [-1, P], [1, STRIP]])
    return eng.dma_start(io["strips"][:, hg * HPG:(hg + 1) * HPG, :].rearrange("p h c -> h p c"), lines)


def load_strips(eng, io, strips, hg):
    return eng.dma_start(strips[:, hg, :, :], io["strips"][:, bass.ds(hg * HPG, HPG), :])


def project_qkv(nc, io, strips):
    with ExitStack() as ctx:
        def sb(name, shape, dt=F32):
            return ctx.enter_context(nc.sbuf_tensor("qp_" + name, shape, dt))

        def sem(name):
            return ctx.enter_context(nc.semaphore("qp_" + name))

        x = [sb(f"x{i}", [P, KT, CH]) for i in range(2)]
        w = sb("w", [P, KT, 3 * D])
        members = sb("members", [P, 8], BF16)
        parts = [sb(f"parts{u}", [P, 3, CH], BF16) for u in range(4)]
        rest = [sb(f"rest{u}", [P, CH]) for u in range(4)]
        squares = [sb(f"squares{u}", [P, CH], BF16) for u in range(4)]
        norms = [sb(f"norms{u}", [8, CH], BF16) for u in range(2)]
        v_out = [sb(f"v_out{i}", [P, 2, H, 32]) for i in range(2)]
        k_peak = sb("k_peak", [P, NCH * 2])
        k_max = sb("k_max", [P, 4])
        ps_u = [ctx.enter_context(nc.psum_tensor(f"qp_ps{u}", [P, CH], F32)) for u in range(6)]
        ps_n = [ctx.enter_context(nc.psum_tensor(f"qp_norm{u}", [8, CH], F32)) for u in range(2)]
        x_loaded = [sem(f"x_loaded{i}") for i in range(2)]
        w_loaded, init_done = sem("w_loaded"), sem("init_done")
        qk_ready, v_ready, norm_ready = sem("qk_ready"), sem("v_ready"), sem("norm_ready")
        hi_done, sq_done, rest_done, mid_done, lo_done = (
            sem(n) for n in ("hi_done", "sq_done", "rest_done", "mid_done", "lo_done"))
        root_done, peak_done, v_copied = sem("root_done"), sem("peak_done"), sem("v_copied")
        unit_stored = [sem(f"unit_stored{u}") for u in range(4)]
        v_stored = [sem(f"v_stored{i}") for i in range(2)]
        kmax_steps = sem("kmax_steps")
        kmax_stored = sem("kmax_stored")
        skewed, strips_loaded = sem("skewed"), sem("strips_loaded")
        per_unit = [16 * (SLOTS + 1), 16 * (SLOTS + 1), 16 * SLOTS, 16 * SLOTS]
        block = ctx.enter_context(nc.Block())

        xT = io["xT"].rearrange("(k p) t -> p k t", p=P)

        @block.sync
        def _(sp):
            sp.dma_start(members[:, :], io["members"]).then_inc(w_loaded, 16)
            sp.dma_start(w[:, :, :], io["wqkvT"].rearrange("(k p) e -> p k e", p=P)).then_inc(w_loaded, 16)
            for i in range(2):
                sp.dma_start(x[i][:, :, :], xT[:, :, i * CH:(i + 1) * CH]).then_inc(x_loaded[i], 16)

            def store(c, i):
                for u in range(4):
                    dst = (io["qstack"] if u < 2 else io["kstack"])[u % 2]
                    which = Q_PARTS if u < 2 else K_PARTS
                    for part, ready in ((0, hi_done), (1, mid_done), (2, lo_done)):
                        sp.wait_ge(ready, 4 * c + u + 1)
                        for slot in range(SLOTS):
                            if which[slot] == part:
                                sp.dma_start(dst[slot * P:(slot + 1) * P, bass.ts(c, CH)],
                                             parts[u][:, part, :]).then_inc(unit_stored[u], 16)
                    if u < 2:
                        sp.wait_ge(root_done, 2 * c + u + 1)
                        sp.dma_start(dst[NORM_ROW * 8:NORM_ROW * 8 + 8, bass.ts(c, CH)],
                                     norms[u][:, :]).then_inc(unit_stored[u], 16)
                for n in range(2):
                    sp.wait_ge(v_copied, 1 + 2 * c + n + 1)
                    rows = io["vpad"][bass.ds(c * CH + n * 2 * P, 2 * P), :]
                    sp.dma_start(rows.rearrange("(t p) e -> p t e", p=P),
                                 v_out[n][:, :, :, :].rearrange("p t h e -> p t (h e)")).then_inc(v_stored[n], 16)

            with sp.Fori(0, NCH // 2 - 1) as pair:
                for i in range(2):
                    c0 = 2 * pair
                    store(c0 + i, i)
                    sp.dma_start(x[i][:, :, :], xT[:, :, bass.ts(c0 + i + 2, CH)]).then_inc(x_loaded[i], 16)
            for i in range(2):
                store(NCH - 2 + i, i)
            sp.wait_ge(kmax_steps, 5)
            sp.dma_start(io["kmax"], k_max[:, 3:4]).then_inc(kmax_stored, 16)
            sp.wait_ge(kmax_stored, 16)
            for u in range(4):
                sp.wait_ge(unit_stored[u], 1 + per_unit[u] * NCH)
            for n in range(2):
                sp.wait_ge(v_stored[n], 1 + 16 * NCH)

        @block.tensor
        def _(pe):
            for free in (peak_done, sq_done, rest_done, v_copied):
                pe.sem_inc(free, 1)
            pe.wait_ge(w_loaded, 32)

            def norm(c, u):
                pe.wait_ge(sq_done, 1 + 4 * c + u + 1)
                if u < 2:
                    pe.wait_ge(peak_done, 1 + 2 * c)
                else:
                    pe.wait_ge(root_done, 2 * c + u - 1)
                nc.tensor.matmul(ps_n[u % 2][:, :], members[:, :], squares[u][:, :],
                                 start=True, stop=True).then_inc(norm_ready, 1)

            with pe.Fori(0, NCH // 2) as pair:
                for i in range(2):
                    c = 2 * pair + i
                    pe.wait_ge(x_loaded[i], 16 * pair + 16)
                    for u in range(4):
                        pe.wait_ge(sq_done, 1 + 4 * c)
                        pe.wait_ge(rest_done, 1 + 4 * c)
                        for k in range(KT):
                            last = nc.tensor.matmul(ps_u[u][:, :], w[:, k, u * P:(u + 1) * P], x[i][:, k, :],
                                                    start=(k == 0), stop=(k == KT - 1))
                        last.then_inc(qk_ready, 1)
                        if u >= 1:
                            norm(c, u - 1)
                    for n in range(2):
                        pe.wait_ge(v_copied, 1 + 2 * c)
                        for t in range(2):
                            for k in range(KT):
                                tok = (2 * n + t) * P
                                last = nc.tensor.matmul(ps_u[4 + n][:, t * D:(t + 1) * D], x[i][:, k, tok:tok + P],
                                                        w[:, k, 2 * D:3 * D], start=(k == 0), stop=(k == KT - 1))
                        last.then_inc(v_ready, 1)
                        if n == 0:
                            norm(c, 3)

        @block.scalar
        def _(act):
            for u in range(4):
                act.sem_inc(unit_stored[u], 1)
            def finish(c, u):
                act.wait_ge(rest_done, 1 + 4 * c + u + 1)
                nc.scalar.activation(parts[u][:, 1, :], rest[u][:, :], ACT.Copy).then_inc(mid_done, 1)
                if u < 2:
                    act.wait_ge(norm_ready, 4 * c + u + 1)
                    nc.scalar.activation(norms[u][:, :], ps_n[u % 2][:, :], ACT.Sqrt).then_inc(root_done, 1)

            with act.Fori(0, NCH, 1) as c:
                for u in range(4):
                    act.wait_ge(qk_ready, 4 * c + u + 1)
                    act.wait_ge(unit_stored[u], 1 + per_unit[u] * c)
                    nc.scalar.activation(parts[u][:, 0, :], ps_u[u][:, :], ACT.Copy).then_inc(hi_done, 1)
                    nc.scalar.activation(squares[u][:, :], ps_u[u][:, :], ACT.Square).then_inc(sq_done, 1)
                    if u >= 1:
                        finish(c, u - 1)
                finish(c, 3)
            act.wait_ge(kmax_steps, 3)
            nc.scalar.activation(k_max[:, 2:3], k_max[:, 1:2], ACT.Sqrt).then_inc(kmax_steps, 1)

        @block.vector
        def _(dve):
            for n in range(2):
                dve.sem_inc(v_stored[n], 1)
            nc.vector.memset(k_max[:, :], 0.0).then_inc(kmax_steps, 1)
            for n in range(2):
                nc.vector.memset(v_out[n][:, :, :, HD:32], 1.0).then_inc(init_done, 1)
            with dve.Fori(0, NCH, 1) as c:
                for u in range(4):
                    dve.wait_ge(sq_done, 1 + 4 * c + u + 1)
                    nc.vector.tensor_tensor(rest[u][:, :], ps_u[u][:, :], parts[u][:, 0, :],
                                            ALU.subtract).then_inc(rest_done, 1)
                for n in range(2):
                    dve.wait_ge(v_ready, 2 * c + n + 1)
                    dve.wait_ge(v_stored[n], 1 + 16 * c)
                    nc.vector.tensor_copy(v_out[n][:, :, :, 0:HD],
                                          ps_u[4 + n][:, :].rearrange("p (t h e) -> p t h e", t=2, h=H)
                                          ).then_inc(v_copied, 1)
                for u in range(2):
                    dve.wait_ge(norm_ready, 4 * c + 2 + u + 1)
                    nc.vector.reduce_max(k_peak[0:8, bass.ds(2 * c + u, 1)], ps_n[u][:, :], AXX).then_inc(peak_done, 1)
            dve.wait_ge(peak_done, 1 + 2 * NCH)
            nc.vector.reduce_max(k_max[0:8, 0:1], k_peak[0:8, :], AXX).then_inc(kmax_steps, 1)
            dve.wait_ge(kmax_steps, 4)
            nc.vector.tensor_scalar(k_max[:, 3:4], k_max[:, 2:3], -1.05, None, ALU.mult).then_inc(kmax_steps, 1)

        @block.gpsimd
        def _(pool):
            skew(pool, io, 0).then_inc(skewed, 16)
            def low_parts(c):
                for u in range(4):
                    pool.wait_ge(mid_done, 4 * c + u + 1)
                    nc.gpsimd.tensor_tensor(parts[u][:, 2, :], rest[u][:, :], parts[u][:, 1, :],
                                            ALU.subtract).then_inc(lo_done, 1)

            with pool.Fori(0, NCH // 2) as c:
                low_parts(c)
            pool.wait_ge(skewed, 16)
            load_strips(pool, io, strips, 0).then_inc(strips_loaded, 16)
            with pool.Fori(0, NCH // 2) as c:
                low_parts(c + NCH // 2)
            pool.wait_ge(kmax_steps, 2)
            nc.gpsimd.partition_all_reduce(k_max[:, 1:2], k_max[:, 0:1], P, RMAX).then_inc(kmax_steps, 1)
            pool.wait_ge(strips_loaded, 16)


def self_attention(nc, io, strips):
    with ExitStack() as ctx:
        def sb(name, shape, dt=F32):
            return ctx.enter_context(nc.sbuf_tensor("sa_" + name, shape, dt))

        def sem(name):
            return ctx.enter_context(nc.semaphore("sa_" + name))

        RING = 4
        q = [sb(f"q{i}", [ROWS + 1, HPG, S], BF16) for i in range(2)]
        k = [sb(f"k{i}", [ROWS + 1, HPG, S], BF16) for i in range(2)]
        v = [sb(f"v{i}", [P, JT, P]) for i in range(2)]
        probs = [sb(f"probs{i}", [P, HPG, CH]) for i in range(RING)]
        o_out = [sb(f"o_out{i}", [P, CH]) for i in range(2)]
        k_max = sb("k_max", [P, 1])
        ones = sb("ones", [P, S], BF16)
        ps_s = [ctx.enter_context(nc.psum_tensor(f"sa_s{i}", [P, 2, CH], F32)) for i in range(2)]
        ps_o = [ctx.enter_context(nc.psum_tensor(f"sa_o{i}", [P, CH], F32)) for i in range(2)]
        skewed, strips_loaded, ones_set = sem("skewed"), sem("strips_loaded"), sem("ones_set")
        kmax_loaded = sem("kmax_loaded")
        shift_set = sem("shift_set")
        loaded = [sem(f"loaded{i}") for i in range(2)]
        scores_ready, added, exp_done, pv_done = (sem(n) for n in ("scores_ready", "added", "exp_done", "pv_done"))
        o_copied, o_stored, o_free = sem("o_copied"), sem("o_stored"), sem("o_free")
        NS = B * STEPS
        block = ctx.enter_context(nc.Block())

        vsrc = io["vpad"].rearrange("(b j p) (g c) -> b g p j c", j=JT, p=P, c=P)

        def rows_of(stack, hg, b, n):
            return bass.AP(stack.tensor, (hg // 2) * ((ROWS + 1) * 8 * T) + (hg % 2) * (4 * T) + b * S,
                           [[8 * T, n], [T, HPG], [1, S]])

        @block.sync
        def _(sp):
            def load(hg, b):
                i = b % 2
                sp.dma_start(q[i][:, :, :], rows_of(io["qstack"], hg, b, ROWS + 1)).then_inc(loaded[i], 16)
                sp.dma_start(k[i][0:ROWS, :, :], rows_of(io["kstack"], hg, b, ROWS)).then_inc(loaded[i], 16)
                sp.dma_start(v[i][:, :, :], vsrc[b, hg]).then_inc(loaded[i], 16)

            sp.dma_start(k_max[:, :], io["kmax"]).then_inc(kmax_loaded, 16)
            load(0, 0)
            load(0, 1)
            for hg in range(1, HG):
                skew(sp, io, hg).then_inc(skewed, 16)
            with sp.Fori(0, HG - 1) as hg:
                for b in (2, 3):
                    sp.wait_ge(pv_done, 1 + hg * NS + STEPS * (b - 1))
                    load(hg, b)
                sp.wait_ge(skewed, 16 * (HG - 1))
                load_strips(sp, io, strips, hg + 1).then_inc(strips_loaded, 16)
                for b in (0, 1):
                    sp.wait_ge(pv_done, 1 + hg * NS + STEPS * (b + 3))
                    load(hg + 1, b)
            for b in (2, 3):
                sp.wait_ge(pv_done, 1 + (HG - 1) * NS + STEPS * (b - 1))
                load(HG - 1, b)

        @block.tensor
        def _(pe):
            pe.sem_inc(o_copied, 1)
            pe.wait_ge(shift_set, 2 * HPG)

            def scores(hg, t):
                b, ih, jt = t // STEPS, (t // JT) % IH, t % JT
                if t % STEPS == 0:
                    pe.wait_ge(loaded[b % 2], 48 * (2 * hg + b // 2) + 48)
                for half in range(2):
                    if t > 0:
                        pe.wait_ge(added, 2 * (hg * NS + t) + half - 1)
                    for n in range(2):
                        h = 2 * half + n
                        last = nc.tensor.matmul(ps_s[half][:, n, :], k[b % 2][:, h, jt * P:(jt + 1) * P],
                                                q[b % 2][:, h, ih * CH:(ih + 1) * CH], start=True, stop=True)
                    last.then_inc(scores_ready, 1)

            def values(hg, t):
                b, ih, jt = t // STEPS, (t // JT) % IH, t % JT
                if jt == 0:
                    pe.wait_ge(o_copied, 1 + hg * 2 * B + max(2 * b + ih - 1, 0))
                pe.wait_ge(exp_done, hg * NS + t + 1)
                for h in range(HPG):
                    last = nc.tensor.matmul(ps_o[ih][32 * h:32 * h + 32, :], v[b % 2][:, jt, 32 * h:32 * h + 32],
                                            probs[t % RING][:, h, :], start=(jt == 0), stop=(jt == JT - 1))
                last.then_inc(pv_done, 1)

            LAG = 2
            with pe.Fori(0, HG) as hg:
                for t in range(NS + LAG):
                    if t < NS:
                        scores(hg, t)
                    if t >= LAG:
                        values(hg, t - LAG)

        @block.vector
        def _(dve):
            dve.sem_inc(pv_done, 1)
            dve.sem_inc(strips_loaded, 1)
            nc.vector.memset(ones[ROWS:ROWS + 1, :], 1.0).then_inc(ones_set, 1)
            dve.wait_ge(kmax_loaded, 16)
            dve.wait_ge(ones_set, 1)
            for i in range(2):
                for h in range(HPG):
                    nc.vector.tensor_scalar(k[i][ROWS:ROWS + 1, h, :], ones[ROWS:ROWS + 1, :],
                                            k_max[ROWS:ROWS + 1, 0:1], None, ALU.mult).then_inc(shift_set, 1)
            with dve.Fori(0, HG) as hg:
                dve.wait_ge(strips_loaded, 1 + 16 * hg)
                for t in range(NS):
                    ih, jt = (t // JT) % IH, t % JT
                    c0 = ih * CH + (JT - 1 - jt) * P
                    if t >= RING:
                        dve.wait_ge(pv_done, 1 + hg * NS + t - RING + 1)
                    else:
                        dve.wait_ge(pv_done, 1 + hg * NS)
                    for half in range(2):
                        dve.wait_ge(scores_ready, 2 * (hg * NS + t) + half + 1)
                        nc.vector.tensor_tensor(probs[t % RING][:, 2 * half:2 * half + 2, :], ps_s[half][:, :, :],
                                                strips[:, hg, 2 * half:2 * half + 2, c0:c0 + CH],
                                                ALU.add).then_inc(added, 1)

        @block.scalar
        def _(act):
            act.sem_inc(o_free, 2)
            def copy_out(hg, n):
                act.wait_ge(pv_done, 1 + hg * NS + JT * (n + 1))
                act.wait_ge(o_free, 1 + hg * 2 * B + n)
                nc.scalar.activation(o_out[n % 2][:, :], ps_o[n % 2][:, :], ACT.Copy).then_inc(o_copied, 1)

            with act.Fori(0, HG) as hg:
                for t in range(NS):
                    act.wait_ge(added, 2 * (hg * NS + t) + 2)
                    nc.scalar.activation(probs[t % RING][:, :, :], probs[t % RING][:, :, :], ACT.Exp,
                                         scale=0.25).then_inc(exp_done, 1)
                    if t % JT == 3 and t > JT:
                        copy_out(hg, t // JT - 1)
                copy_out(hg, NS // JT - 1)

        @block.gpsimd
        def _(pool):
            with pool.Fori(0, HG) as hg:
                for n in range(2 * B):
                    pool.wait_ge(o_copied, 1 + hg * 2 * B + n + 1)
                    pool.dma_start(io["oT"][hg, :, n * CH:(n + 1) * CH], o_out[n % 2][:, :]).then_inc(o_stored, 16)
                    pool.wait_ge(o_stored, 16 * (hg * 2 * B + n + 1))
                    pool.sem_inc(o_free, 1)


def check_and_exact_attention(nc, io, strips):
    with ExitStack() as ctx:
        def sb(name, shape, dt=F32):
            return ctx.enter_context(nc.sbuf_tensor("ex_" + name, shape, dt))

        def sem(name):
            return ctx.enter_context(nc.semaphore("ex_" + name))

        den = sb("den", [P, CH])
        rec = sb("rec", [P, CH])
        low = sb("low", [P, 4])
        flag = sb("flag", [P, 1], I32)
        oT_heads = io["oT"].rearrange("g (h r) t -> (g h) r t", r=32)

        def load_dens(eng, done):
            for n in range(NCH):
                eng.dma_start(den[n * H:(n + 1) * H, :], oT_heads[:, HD, n * CH:(n + 1) * CH]).then_inc(done, 16)

        def store_recs(eng, done):
            for n in range(NCH):
                eng.dma_start(io["rec"][:, n * CH:(n + 1) * CH], rec[n * H:(n + 1) * H, :]).then_inc(done, 16)

        with ExitStack() as inner:
            def sem_a(name):
                return inner.enter_context(nc.semaphore("ck_" + name))

            den_loaded, rec_stored, rec_done, steps = (
                sem_a(n) for n in ("den_loaded", "rec_stored", "rec_done", "steps"))
            block = inner.enter_context(nc.Block())

            @block.sync
            def _(sp):
                load_dens(sp, den_loaded)
                sp.wait_ge(rec_done, 1)
                store_recs(sp, rec_stored)
                sp.wait_ge(rec_stored, 16 * NCH)

            @block.vector
            def _(dve):
                dve.wait_ge(den_loaded, 16 * NCH)
                nc.vector.tensor_reduce(low[:, 0:1], den[:, :], AXX, ALU.min).then_inc(steps, 1)
                dve.wait_ge(steps, 1)
                nc.vector.tensor_scalar(low[:, 1:2], low[:, 0:1], -1.0, None, ALU.mult).then_inc(steps, 1)
                nc.vector.reciprocal(rec[:, :], den[:, :]).then_inc(rec_done, 1)
                dve.wait_ge(steps, 3)
                nc.vector.tensor_scalar(low[:, 3:4], low[:, 2:3], -TINY, 0.0, ALU.is_le, ALU.is_equal).then_inc(steps, 1)
                dve.wait_ge(steps, 4)
                nc.vector.tensor_copy(flag[:, :], low[:, 3:4]).then_inc(steps, 1)

            @block.gpsimd
            def _(pool):
                pool.wait_ge(steps, 2)
                nc.gpsimd.partition_all_reduce(low[:, 2:3], low[:, 1:2], P, RMAX).then_inc(steps, 1)

        SPLIT = 3
        q = sb("q", [ROWS + SPLIT, HPG, S], BF16)
        k = sb("k", [ROWS + SPLIT, HPG, S], BF16)
        v = sb("v", [P, JT, P])
        work = sb("work", [P, HPG, CH])
        o_out = sb("o_out", [P, CH])
        ident = sb("ident", [P, P])
        peaks = sb("peaks", [P, HPG * JT])
        shift = sb("shift", [HPG * JT, 2, P])
        shift_parts = sb("shift_parts", [HPG * JT, SPLIT, P], BF16)
        ps_s = [ctx.enter_context(nc.psum_tensor(f"ex_s{i}", [P, 2, CH], F32)) for i in range(2)]
        ps_o = [ctx.enter_context(nc.psum_tensor(f"ex_o{i}", [P, CH], F32)) for i in range(2)]
        ps_t = ctx.enter_context(nc.psum_tensor("ex_t", [HPG * JT, P], F32))
        (ident_loaded, loaded, ones_set, logits_ready, logits_added, maxed, turned, shift_ready,
         shift_loaded, scores_ready, added, exp_done, pv_done, o_copied, o_stored, den_loaded, rec_done,
         rec_stored) = (sem(n) for n in (
             "ident_loaded", "loaded", "ones_set", "logits_ready", "logits_added", "maxed", "turned",
             "shift_ready", "shift_loaded", "scores_ready", "added", "exp_done", "pv_done", "o_copied", "o_stored",
             "den_loaded", "rec_done", "rec_stored"))
        split_steps = sem("split_steps")
        NM = HPG * JT
        block = ctx.enter_context(nc.Block())

        def rows_of(stack, hg, b):
            return bass.AP(stack.tensor, (hg // 2) * ((ROWS + 1) * 8 * T) + (hg % 2) * (4 * T) + b * S,
                           [[8 * T, ROWS], [T, HPG], [1, S]])

        @block.sync
        def _(sp):
            needed = sp.value_load(flag[0:1, 0:1], min_val=0, max_val=1)
            with sp.If(needed > 0):
                sp.sem_inc(pv_done, 1)
                sp.dma_start(ident[:, :], io["ident"]).then_inc(ident_loaded, 16)
                with sp.Fori(0, HG) as hg:
                    with sp.Fori(0, B) as b:
                        g = hg * B + b
                        sp.wait_ge(pv_done, 1 + g * STEPS)
                        sp.dma_start(q[0:ROWS, :, :], rows_of(io["qstack"], hg, b)).then_inc(loaded, 16)
                        sp.dma_start(k[0:ROWS, :, :], rows_of(io["kstack"], hg, b)).then_inc(loaded, 16)
                        sp.dma_start(v[:, :, :], io["vpad"].rearrange("(b j p) (g c) -> b g p j c", j=JT, p=P, c=P)[b, hg]
                                     ).then_inc(loaded, 16)
                        sp.wait_ge(shift_ready, g + 1)
                        for n in range(SPLIT):
                            sp.dma_start(q[ROWS + n:ROWS + n + 1, :, :].rearrange("p h s -> p (h s)"),
                                         shift_parts[:, n, :]).then_inc(shift_loaded, 16)
                        for ih in range(IH):
                            sp.wait_ge(o_copied, 1 + IH * g + ih + 1)
                            sp.dma_start(io["oT"][hg, :, bass.ds(b * S + ih * CH, CH)], o_out[:, :]).then_inc(o_stored, 16)
                sp.wait_ge(o_stored, 1 + 16 * IH * HG * B)
                load_dens(sp, den_loaded)
                sp.wait_ge(rec_done, 1)
                store_recs(sp, rec_stored)
                sp.wait_ge(rec_stored, 16 * NCH)

        @block.tensor
        def _(pe):
            needed = pe.value_load(flag[0:1, 0:1], min_val=0, max_val=1)
            with pe.If(needed > 0):
                for free in (maxed, added, o_copied):
                    pe.sem_inc(free, 1)
                pe.wait_ge(ident_loaded, 16)
                pe.wait_ge(ones_set, 1)
                with pe.Fori(0, HG * B) as g:
                    pe.wait_ge(loaded, 48 * g + 48)
                    for n in range(NM):
                        h, it = n // JT, n % JT
                        pe.wait_ge(maxed, 1 + NM * g + n)
                        if n == 0:
                            pe.wait_ge(added, 1 + 2 * STEPS * g)
                        for half in range(2):
                            last = nc.tensor.matmul(ps_s[0][:, half, :], q[0:ROWS, h, it * P:(it + 1) * P],
                                                    k[0:ROWS, h, half * CH:(half + 1) * CH], start=True, stop=True)
                        last.then_inc(logits_ready, 1)
                    pe.wait_ge(maxed, 1 + NM * g + NM)
                    nc.tensor.transpose(ps_t[:, :], peaks[:, :], ident[:, :]).then_inc(turned, 1)
                    pe.wait_ge(shift_loaded, 16 * SPLIT * (g + 1))
                    for t in range(STEPS):
                        ih, jt = t // JT, t % JT
                        pe.wait_ge(pv_done, 1 + STEPS * g + t)
                        for h in range(HPG):
                            last = nc.tensor.matmul(ps_s[h // 2][:, h % 2, :], k[:, h, jt * P:(jt + 1) * P],
                                                    q[:, h, ih * CH:(ih + 1) * CH], start=True, stop=True)
                            if h % 2:
                                last.then_inc(scores_ready, 1)
                        pe.wait_ge(exp_done, STEPS * g + t + 1)
                        if jt == 0:
                            pe.wait_ge(o_copied, 1 + IH * g + ih)
                        for h in range(HPG):
                            last = nc.tensor.matmul(ps_o[ih][32 * h:32 * h + 32, :], v[:, jt, 32 * h:32 * h + 32],
                                                    work[:, h, :], start=(jt == 0), stop=(jt == JT - 1))
                        last.then_inc(pv_done, 1)

        @block.vector
        def _(dve):
            needed = dve.value_load(flag[0:1, 0:1], min_val=0, max_val=1)
            with dve.If(needed > 0):
                nc.vector.memset(k[ROWS:ROWS + SPLIT, :, :], 1.0).then_inc(ones_set, 1)
                with dve.Fori(0, HG) as hg:
                    with dve.Fori(0, B) as b:
                        g = hg * B + b
                        for n in range(NM):
                            h, it = n // JT, n % JT
                            dve.wait_ge(logits_ready, NM * g + n + 1)
                            c0 = (JT - 1 - it) * P
                            nc.vector.tensor_tensor(work[:, 0:2, :].rearrange("p a c -> p (a c)"),
                                                    ps_s[0][:, :, :].rearrange("p a c -> p (a c)"),
                                                    strips[:, hg, h, c0:c0 + S], ALU.add).then_inc(logits_added, 1)
                            dve.wait_ge(logits_added, NM * g + n + 1)
                            nc.vector.reduce_max(peaks[:, n:n + 1], work[:, 0:2, :].rearrange("p a c -> p (a c)"),
                                                 AXX).then_inc(maxed, 1)
                        dve.wait_ge(turned, g + 1)
                        nc.vector.tensor_scalar(shift[:, 0, :], ps_t[:, :], -1.0, None, ALU.mult).then_inc(split_steps, 1)
                        dve.wait_ge(split_steps, 5 * g + 1)
                        nc.vector.tensor_copy(shift_parts[:, 0, :], shift[:, 0, :]).then_inc(split_steps, 1)
                        dve.wait_ge(split_steps, 5 * g + 2)
                        nc.vector.tensor_tensor(shift[:, 1, :], shift[:, 0, :], shift_parts[:, 0, :],
                                                ALU.subtract).then_inc(split_steps, 1)
                        dve.wait_ge(split_steps, 5 * g + 3)
                        nc.vector.tensor_copy(shift_parts[:, 1, :], shift[:, 1, :]).then_inc(split_steps, 1)
                        dve.wait_ge(split_steps, 5 * g + 4)
                        nc.vector.tensor_tensor(shift[:, 0, :], shift[:, 1, :], shift_parts[:, 1, :],
                                                ALU.subtract).then_inc(split_steps, 1)
                        dve.wait_ge(split_steps, 5 * g + 5)
                        nc.vector.tensor_copy(shift_parts[:, 2, :], shift[:, 0, :]).then_inc(shift_ready, 1)
                        for t in range(STEPS):
                            ih, jt = t // JT, t % JT
                            c0 = ih * CH + (JT - 1 - jt) * P
                            for half in range(2):
                                dve.wait_ge(scores_ready, 2 * (STEPS * g + t) + half + 1)
                                nc.vector.tensor_tensor(work[:, 2 * half:2 * half + 2, :], ps_s[half][:, :, :],
                                                        strips[:, hg, 2 * half:2 * half + 2, c0:c0 + CH],
                                                        ALU.add).then_inc(added, 1)
                dve.wait_ge(den_loaded, 16 * NCH)
                nc.vector.reciprocal(rec[:, :], den[:, :]).then_inc(rec_done, 1)

        @block.scalar
        def _(act):
            needed = act.value_load(flag[0:1, 0:1], min_val=0, max_val=1)
            with act.If(needed > 0):
                act.sem_inc(o_stored, 1)
                with act.Fori(0, HG * B) as g:
                    for t in range(STEPS):
                        act.wait_ge(added, 1 + 2 * (STEPS * g + t) + 2)
                        nc.scalar.activation(work[:, :, :], work[:, :, :], ACT.Exp, scale=0.25).then_inc(exp_done, 1)
                        if t % JT == JT - 1:
                            n = t // JT
                            act.wait_ge(pv_done, 1 + STEPS * g + t + 1)
                            act.wait_ge(o_stored, 1 + 16 * (IH * g + n))
                            nc.scalar.activation(o_out[:, :], ps_o[n][:, :], ACT.Copy).then_inc(o_copied, 1)


NK, CD = 77, 192
NKB = HPG * NK
TT = CH // P
NTT = T // P
E_, HID, R = 8, 512, 16
EPS = 1e-5


def moments_of(dve, nc, stats_done, stats_count, stats, moments, halves_done, before, done):
    gap = moments[:, :, 2]
    spread = moments[:, :, 3]
    dve.wait_ge(stats_done, stats_count)
    nc.vector.tensor_tensor(gap, stats[:, :, 1], stats[:, :, 4], ALU.subtract).then_inc(halves_done, 1)
    nc.vector.tensor_tensor(moments[:, :, 0:2], stats[:, :, 1:3], stats[:, :, 4:6], ALU.add).then_inc(halves_done, 1)
    dve.wait_ge(halves_done, before + 1)
    nc.vector.scalar_tensor_tensor(out=spread, in0=gap, scalar=0.25, in1=gap, op0=ALU.mult,
                                   op1=ALU.mult).then_inc(halves_done, 1)
    dve.wait_ge(halves_done, before + 3)
    nc.vector.tensor_scalar(moments[:, :, 0], moments[:, :, 0], 0.5, None, ALU.mult).then_inc(halves_done, 1)
    nc.vector.scalar_tensor_tensor(out=moments[:, :, 1], in0=moments[:, :, 1], scalar=1.0 / D, in1=spread,
                                   op0=ALU.mult, op1=ALU.add).then_inc(done, 1)


def cross_block(nc, io, x2_all, logits):
    with ExitStack() as ctx:
        def sb(name, shape, dt=F32):
            return ctx.enter_context(nc.sbuf_tensor("cb_" + name, shape, dt))

        def sem(name):
            return ctx.enter_context(nc.semaphore("cb_" + name))

        wout = sb("wout", [P, KT, D])
        wq = sb("wq", [P, KT, D])
        wg = sb("wg", [P, KT, E_])
        ident = sb("ident", [P, P])
        block8 = sb("block8", [P, 8])
        mask8 = sb("mask8", [P, NTT], U8)
        mask = sb("mask", [P, NTT])
        mask_now = [sb(f"mask_now{i}", [P, TT]) for i in range(2)]
        exponent = sb("exponent", [P, TT])
        eps = sb("eps", [P, TT])
        ctx_a = sb("ctx_a", [P, B * NK])
        ctx_b = sb("ctx_b", [CD - P, B * NK])
        wkv_a = sb("wkv_a", [P, 2 * D])
        wkv_b = sb("wkv_b", [CD - P, 2 * D])
        k_rows = sb("k_rows", [P, KT, B * NK])
        k_diag = sb("k_diag", [P, KT, B, 8 * NK])
        v_all = sb("v_all", [NK, B, H * 32])
        v_now = [sb(f"v_now{i}", [NK, H * 32]) for i in range(2)]
        oc = [sb(f"oc{i}", [P, KT, CH]) for i in range(2)]
        recb = [sb(f"recb{i}", [P, KT, CH]) for i in range(2)]
        x1 = [sb(f"x1{i}", [P, TT, D]) for i in range(2)]
        x1m = [sb(f"x1m{i}", [P, TT, D]) for i in range(2)]
        x2 = [sb(f"x2{i}", [P, TT, D]) for i in range(2)]
        x2T = sb("x2T", [P, KT, CH])
        xT = [sb(f"xT{i}", [P, KT, CH]) for i in range(2)]
        qT = [sb(f"qT{i}", [P, KT, CH]) for i in range(2)]
        peak = [sb(f"peak{i}", [P, H]) for i in range(2)]
        probs = [sb(f"probs{i}", [P, H, NK]) for i in range(2)]
        pT = sb("pT", [NK, H, CH])
        oT = sb("oT", [P, HG, CH])
        dinv = sb("dinv", [P, TT, H])
        stats = [sb(f"stats{i}", [P, TT, 6]) for i in range(2)]
        moments = [sb(f"moments{i}", [P, TT, 4]) for i in range(2)]
        rstd = [sb(f"rstd{i}", [P, TT]) for i in range(2)]
        ps_l = [ctx.enter_context(nc.psum_tensor(f"cb_l{i}", [P, 2, 512], F32)) for i in range(2)]
        ps_att = [ctx.enter_context(nc.psum_tensor(f"cb_att{i}", [P, 512], F32)) for i in range(2)]
        ps_pre = ctx.enter_context(nc.psum_tensor("cb_pre", [P, 512], F32))
        ps_post = ctx.enter_context(nc.psum_tensor("cb_post", [P, 512], F32))

        PROJ, X1T, Q, X2T, GATE = 0, 2, 4, 0, 2
        PT, OH, OTOK = 0, 4 * TT, 4 * TT + HG
        PRE, POST, ATT = 6, 3, 4 * TT + HG + TT
        pre_filled, pre_drained, post_filled, post_drained = (
            sem(n) for n in ("pre_filled", "pre_drained", "post_filled", "post_drained"))
        att_filled = [sem(f"att_filled{i}") for i in range(2)]
        att_drained = [sem(f"att_drained{i}") for i in range(2)]
        l_filled = [sem(f"l_filled{i}") for i in range(2)]
        l_drained = [sem(f"l_drained{i}") for i in range(2)]

        def wait(eng, semaphore, value):
            if not (isinstance(value, int) and value <= 0):
                eng.wait_ge(semaphore, value)

        def att_uses(n, use):
            return n * (ATT // 2) + use // 2

        def chunks(eng, first, slot, last):
            first()
            slot(0, 0, 0, after=False)
            with eng.Fori(0, (NCH - 2) // 2) as it:
                slot(2 * it + 1, 1, it)
                slot(2 * it + 2, 0, it + 1)
            slot(NCH - 1, 1, B - 1, before=False)
            last()

        w_loaded = sem("w_loaded")
        o_loaded = [sem(f"o_loaded{i}") for i in range(2)]
        x_loaded = [sem(f"x_loaded{i}") for i in range(2)]
        set_up = sem("set_up")
        SET_UP = 1 + KT + 3 + B * (1 + KT)
        setup_mm = sem("setup_mm")
        v_placed, scaled, mask_placed, kept, placed = (
            sem(n) for n in ("v_placed", "scaled", "mask_placed", "kept", "placed"))
        stat_done, var_done, rstd_done, normed, masked = (
            sem(n) for n in ("stat_done", "var_done", "rstd_done", "normed", "masked"))
        peaked, exp_done = sem("peaked"), sem("exp_done")
        inv_done, halves_done = sem("inv_done"), sem("halves_done")
        summed2, stat2_done, var2_done, rstd2_done, normed2 = (
            sem(n) for n in ("summed2", "stat2_done", "var2_done", "rstd2_done", "normed2"))
        block = ctx.enter_context(nc.Block())

        @block.sync
        def _(sp):
            def load(n, c):
                tok = n * CH
                for k in range(KT):
                    sp.dma_start(oc[c][:, k, :], bass.AP(io["oT"].tensor, tok + k * 2 * P * T,
                                                         [[32 * T, 8], [T, HD], [1, CH]])).then_inc(o_loaded[c], 16)
                    sp.dma_start(recb[c][:, k, :], bass.AP(io["rec"].tensor, tok + k * 8 * T,
                                                           [[T, 8], [0, HD], [1, CH]])).then_inc(o_loaded[c], 16)

            def load_x(n, c):
                sp.dma_start(x1[c][:, :, :], io["x"][bass.ds(n * CH, CH), :].rearrange(
                    "(t p) d -> p t d", p=P)).then_inc(x_loaded[c], 16)

            for dst, name in ((ctx_a, "ctxT_a"), (ctx_b, "ctxT_b"), (wkv_a, "wkvT_a"), (wkv_b, "wkvT_b"),
                              (block8, "block8"), (ident, "ident"), (mask8, "mask")):
                sp.dma_start(dst[:, :], io[name]).then_inc(w_loaded, 16)
            for dst, name in ((wout, "woutT"), (wq, "wqT"), (wg, "wgT")):
                sp.dma_start(dst[:, :, :], io[name].rearrange("(k p) e -> p k e", p=P)).then_inc(w_loaded, 16)
            for c in range(2):
                load(c, c)
                load_x(c, c)
            with sp.Fori(0, NCH // 2 - 1) as it:
                for c in range(2):
                    n = 2 * it + c
                    sp.wait_ge(pre_filled, PRE * n + PROJ + 2)
                    load(n + 2, c)
                    sp.wait_ge(kept, n + 1)
                    load_x(n + 2, c)

        @block.tensor
        def _(pe):
            pe.wait_ge(w_loaded, 160)
            for k in range(KT):
                nc.tensor.matmul(ps_att[k][:, 0:B * NK], wkv_a[:, k * P:(k + 1) * P], ctx_a[:, :],
                                 start=True, stop=False)
                nc.tensor.matmul(ps_att[k][:, 0:B * NK], wkv_b[:, k * P:(k + 1) * P], ctx_b[:, :],
                                 start=False, stop=True).then_inc(setup_mm, 1)
            for b in range(B):
                out = ps_l[b // 2][:NK, b % 2, 0:D]
                nc.tensor.matmul(out, ctx_a[:, b * NK:(b + 1) * NK], wkv_a[:, D:2 * D], start=True, stop=False)
                nc.tensor.matmul(out, ctx_b[:, b * NK:(b + 1) * NK], wkv_b[:, D:2 * D],
                                 start=False, stop=True).then_inc(setup_mm, 1)
            pe.wait_ge(set_up, SET_UP)

            def project(n, c, half):
                if half == 0:
                    pe.wait_ge(scaled, n + 1)
                wait(pe, pre_drained, PRE * n + PROJ + half)
                for t in (2 * half, 2 * half + 1):
                    for k in range(KT):
                        last = nc.tensor.matmul(ps_pre[:, t % 2 * D:(t % 2 + 1) * D], oc[c][:, k, t * P:(t + 1) * P],
                                                wout[:, k, :], start=(k == 0), stop=(k == KT - 1))
                last.then_inc(pre_filled, 1)

            def turn_x1(n, c):
                pe.wait_ge(masked, n + 1)
                for k in range(KT):
                    pe.wait_ge(pre_drained, PRE * n + X1T + k)
                    for t in range(TT):
                        last = nc.tensor.transpose(ps_pre[:, t * P:(t + 1) * P], x1m[c][:, t, k * P:(k + 1) * P],
                                                   ident[:, :])
                    last.then_inc(pre_filled, 1)

            def queries(n, c):
                for m in range(KT):
                    pe.wait_ge(pre_drained, PRE * n + Q + m)
                    for k in range(KT):
                        last = nc.tensor.matmul(ps_pre[:, :], wq[:, k, m * P:(m + 1) * P], xT[c][:, k, :],
                                                start=(k == 0), stop=(k == KT - 1))
                    last.then_inc(pre_filled, 1)

            def logits_of(n, c, b, t):
                for k in range(KT):
                    if t == 0:
                        pe.wait_ge(pre_drained, PRE * n + Q + k + 1)
                    wait(pe, l_drained[k], TT * n + t)
                    for half in range(2):
                        last = nc.tensor.matmul(ps_l[k][:, half, 0:NKB], qT[c][:, k, t * P:(t + 1) * P],
                                                k_diag[:, k, b, half * NKB:(half + 1) * NKB], start=True, stop=True)
                    last.then_inc(l_filled[k], 1)

            def turn_probs(n, t):
                pe.wait_ge(exp_done, TT * n + t + 1)
                for m in range(4):
                    use = PT + 4 * t + m
                    wait(pe, att_drained[use % 2], att_uses(n, use))
                    for h in range(4):
                        last = nc.tensor.transpose(ps_att[use % 2][:NK, h * P:(h + 1) * P],
                                                   probs[t % 2][:, 4 * m + h, :], ident[:, :])
                    last.then_inc(att_filled[use % 2], 1)

            def outputs(n, c):
                pe.wait_ge(v_placed, n + 1)
                for g in range(HG):
                    use = OH + g
                    wait(pe, att_drained[use % 2], att_uses(n, use))
                    if g == 0:
                        wait(pe, att_drained[1], att_uses(n, PT + 4 * TT - 1) + 1)
                    for h in range(HPG):
                        last = nc.tensor.matmul(ps_att[use % 2][32 * h:32 * h + 32, :],
                                                v_now[c][:, (4 * g + h) * 32:(4 * g + h + 1) * 32],
                                                pT[:, 4 * g + h, :], start=True, stop=True)
                    last.then_inc(att_filled[use % 2], 1)
                pe.wait_ge(att_drained[1], att_uses(n, OH + HG - 1) + 1)
                for s in range(TT):
                    use = OTOK + s
                    pe.wait_ge(att_drained[use % 2], att_uses(n, use))
                    for g in range(HG):
                        last = nc.tensor.transpose(ps_att[use % 2][:, g * P:(g + 1) * P],
                                                   oT[:, g, s * P:(s + 1) * P], ident[:, :])
                    last.then_inc(att_filled[use % 2], 1)

            def turn_x2(n, c):
                pe.wait_ge(normed2, TT * (n + 1))
                for k in range(KT):
                    pe.wait_ge(post_drained, 1 + POST * n + X2T + k)
                    for t in range(TT):
                        last = nc.tensor.transpose(ps_post[:, t * P:(t + 1) * P], x2[c][:, t, k * P:(k + 1) * P],
                                                   ident[:, :])
                    last.then_inc(post_filled, 1)

            def gate(n):
                pe.wait_ge(post_drained, 1 + POST * n + GATE)
                for t in range(TT):
                    for k in range(KT):
                        last = nc.tensor.matmul(ps_post[:, t * E_:(t + 1) * E_], x2T[:, k, t * P:(t + 1) * P],
                                                wg[:, k, :], start=(k == 0), stop=(k == KT - 1))
                last.then_inc(post_filled, 1)

            def first():
                project(0, 0, 0)
                project(0, 0, 1)
                turn_x1(0, 0)
                queries(0, 0)
                logits_of(0, 0, 0, 0)

            def slot(n, c, b, before=True, after=True):
                logits_of(n, c, b, 1)
                if before:
                    project(n + 1, 1 - c, 0)
                turn_probs(n, 0)
                logits_of(n, c, b, 2)
                if before:
                    project(n + 1, 1 - c, 1)
                turn_probs(n, 1)
                logits_of(n, c, b, 3)
                if after:
                    turn_x2(n - 1, 1 - c)
                turn_probs(n, 2)
                if after:
                    gate(n - 1)
                if before:
                    turn_x1(n + 1, 1 - c)
                turn_probs(n, 3)
                if before:
                    queries(n + 1, 1 - c)
                    logits_of(n + 1, 1 - c, b + c, 0)
                outputs(n, c)

            def last():
                turn_x2(NCH - 1, 1)
                gate(NCH - 1)

            chunks(pe, first, slot, last)

        @block.scalar
        def _(act):
            def copy(out, src, filled, count, drained, scale=1.0):
                act.wait_ge(filled, count)
                nc.scalar.activation(out, src, ACT.Copy, scale=scale).then_inc(drained, 1)

            def copy_x1(n, c):
                for k in range(KT):
                    copy(xT[c][:, k, :], ps_pre[:, :], pre_filled, PRE * n + X1T + k + 1, pre_drained)

            def copy_queries(n, c):
                for k in range(KT):
                    copy(qT[c][:, k, :], ps_pre[:, :], pre_filled, PRE * n + Q + k + 1, pre_drained, HD ** -0.5)

            def copy_x2(n):
                for k in range(KT):
                    copy(x2T[:, k, :], ps_post[:, :], post_filled, POST * n + X2T + k + 1, post_drained)

            def exponentials(n, t):
                for k in range(KT):
                    act.wait_ge(l_drained[k], TT * n + t + 1)
                nc.scalar.activation(probs[t % 2][:, :, :], probs[t % 2][:, :, :], ACT.Exp).then_inc(exp_done, 1)

            def copy_probs(n, t):
                for m in range(4):
                    use = PT + 4 * t + m
                    copy(pT[:, 4 * m:4 * m + 4, t * P:(t + 1) * P],
                         ps_att[use % 2][:NK, :].rearrange("p (h t) -> p h t", h=4),
                         att_filled[use % 2], att_uses(n, use) + 1, att_drained[use % 2])

            def copy_outputs(n):
                for g in range(HG):
                    use = OH + g
                    copy(oT[:, g, :], ps_att[use % 2][:, :], att_filled[use % 2], att_uses(n, use) + 1,
                         att_drained[use % 2])

            def first():
                copy_x1(0, 0)
                copy_queries(0, 0)

            def slot(n, c, b, before=True, after=True):
                exponentials(n, 0)
                exponentials(n, 1)
                copy_probs(n, 0)
                exponentials(n, 2)
                copy_probs(n, 1)
                if after:
                    copy_x2(n - 1)
                exponentials(n, 3)
                copy_probs(n, 2)
                if before:
                    copy_x1(n + 1, 1 - c)
                copy_probs(n, 3)
                if before:
                    copy_queries(n + 1, 1 - c)
                copy_outputs(n)

            def last():
                copy_x2(NCH - 1)

            chunks(act, first, slot, last)

        @block.vector
        def _(dve):
            dve.wait_ge(w_loaded, 160)
            dve.sem_inc(placed, 1)
            dve.sem_inc(post_drained, 1)
            nc.vector.tensor_copy(mask[:, :], mask8[:, :]).then_inc(set_up, 1)
            for k in range(KT):
                dve.wait_ge(setup_mm, k + 1)
                nc.vector.tensor_copy(k_rows[:, k, :], ps_att[k][:, 0:B * NK]).then_inc(set_up, 1)
            nc.vector.memset(v_all[:, :, :], 1.0).then_inc(set_up, 1)
            nc.vector.memset(exponent[:, :], -0.5).then_inc(set_up, 1)
            nc.vector.memset(eps[:, :], EPS).then_inc(set_up, 1)
            dve.wait_ge(set_up, 6)
            for b in range(B):
                dve.wait_ge(setup_mm, KT + b + 1)
                nc.vector.tensor_copy(v_all[:, b, :].rearrange("p (h e) -> p h e", e=32)[:, :, 0:HD],
                                      ps_l[b // 2][:NK, b % 2, 0:D].rearrange("p (h e) -> p h e", e=HD)
                                      ).then_inc(set_up, 1)
                for k in range(KT):
                    nc.vector.tensor_tensor(
                        k_diag[:, k, b, :].rearrange("p (h n) -> p h n", h=8),
                        k_rows[:, k, b * NK:(b + 1) * NK].unsqueeze(1).to_broadcast([P, 8, NK]),
                        block8[:, :].unsqueeze(2).to_broadcast([P, 8, NK]), ALU.mult).then_inc(set_up, 1)

            def statistics(n, c, x, moment, s_done, v_done):
                for t in range(TT):
                    nc.vector.bn_stats(stats[c][:, t, :], x[:, t, :]).then_inc(s_done, 1)
                moments_of(dve, nc, s_done, TT * (n + 1), stats[c], moments[c], halves_done, 4 * moment, v_done)

            def normalise(n, c, x, r_done, done):
                dve.wait_ge(r_done, 2 * n + 2)
                for t in range(TT):
                    nc.vector.tensor_scalar(x[:, t, :], x[:, t, :], moments[c][:, t, 0:1], rstd[c][:, t:t + 1],
                                            ALU.subtract, ALU.mult).then_inc(done, 1)

            def add_projection(n, c, b, half):
                if half == 0:
                    dve.wait_ge(x_loaded[c], 16 * b + 16)
                dve.wait_ge(pre_filled, PRE * n + PROJ + half + 1)
                nc.vector.tensor_tensor(x1[c][:, 2 * half:2 * half + 2, :],
                                        ps_pre[:, :].rearrange("p (t d) -> p t d", t=2),
                                        x1[c][:, 2 * half:2 * half + 2, :], ALU.add).then_inc(pre_drained, 1)

            def statistics1(n, c, moment):
                dve.wait_ge(pre_drained, PRE * n + PROJ + 2)
                statistics(n, c, x1[c], moment, stat_done, var_done)

            def shift_logits(n, t):
                if t < 2:
                    wait(dve, att_filled[1], att_uses(n - 1, PT + 4 * (t + 2) + 3) + 1)
                else:
                    dve.wait_ge(att_filled[1], att_uses(n, PT + 4 * (t - 2) + 3) + 1)
                for k in range(KT):
                    src = ps_l[k][:, :, 0:NKB].rearrange("p a (h n) -> p a h n", n=NK)
                    top = peak[t % 2][:, 8 * k:8 * k + 8].rearrange("p (a h) -> p a h", a=2)
                    dve.wait_ge(l_filled[k], TT * n + t + 1)
                    nc.vector.tensor_reduce(top, src, AXX, ALU.max).then_inc(peaked, 1)
                    dve.wait_ge(peaked, KT * (TT * n + t) + k + 1)
                    nc.vector.tensor_tensor(
                        probs[t % 2][:, 8 * k:8 * k + 8, :].rearrange("p (a h) n -> p a h n", a=2), src,
                        top.unsqueeze(3).to_broadcast([P, 2, 4, NK]), ALU.subtract).then_inc(l_drained[k], 1)

            def add_attention(n, c, moment):
                dve.wait_ge(placed, n + 1)
                dve.wait_ge(kept, n + 1)
                for s in range(TT):
                    use = OTOK + s
                    dve.wait_ge(att_filled[use % 2], att_uses(n, use) + 1)
                    src = ps_att[use % 2][:, :].rearrange("p (h e) -> p h e", e=32)
                    nc.vector.reciprocal(dinv[:, s, :], src[:, :, HD]).then_inc(inv_done, 1)
                    dve.wait_ge(inv_done, TT * n + s + 1)
                    nc.vector.tensor_tensor(
                        x2[c][:, s, :].rearrange("p (h e) -> p h e", e=HD), src[:, :, 0:HD],
                        dinv[:, s, :].unsqueeze(2).to_broadcast([P, H, HD]), ALU.mult).then_inc(att_drained[use % 2], 1)
                dve.wait_ge(att_drained[0], att_uses(n, OTOK + TT - 2) + 1)
                dve.wait_ge(att_drained[1], att_uses(n, OTOK + TT - 1) + 1)
                nc.vector.tensor_tensor(x2[c][:, :, :], x2[c][:, :, :], x2_all[:, bass.ds(n * TT, TT), :],
                                        ALU.add).then_inc(summed2, 1)
                dve.wait_ge(summed2, n + 1)
                statistics(n, c, x2[c], moment, stat2_done, var2_done)

            def take_gates(n):
                dve.wait_ge(post_filled, POST * n + GATE + 1)
                nc.vector.tensor_copy(logits[:, bass.ds(n * TT, TT), :],
                                      ps_post[:, 0:TT * E_].rearrange("p (t e) -> p t e", e=E_)).then_inc(post_drained, 1)

            def first():
                add_projection(0, 0, 0, 0)
                add_projection(0, 0, 0, 1)
                statistics1(0, 0, 0)
                normalise(0, 0, x1[0], rstd_done, normed)

            def slot(n, c, b, before=True, after=True):
                shift_logits(n, 0)
                if after:
                    add_attention(n - 1, 1 - c, 2 * n)
                shift_logits(n, 1)
                if before:
                    add_projection(n + 1, 1 - c, b + c, 0)
                if after:
                    normalise(n - 1, 1 - c, x2[1 - c], rstd2_done, normed2)
                shift_logits(n, 2)
                if before:
                    add_projection(n + 1, 1 - c, b + c, 1)
                    statistics1(n + 1, 1 - c, 2 * n + 1)
                shift_logits(n, 3)
                if before:
                    normalise(n + 1, 1 - c, x1[1 - c], rstd_done, normed)
                if after:
                    take_gates(n - 1)

            def last():
                add_attention(NCH - 1, 1, 2 * NCH - 1)
                normalise(NCH - 1, 1, x2[1], rstd2_done, normed2)
                take_gates(NCH - 1)

            chunks(dve, first, slot, last)

        @block.gpsimd
        def _(pool):
            pool.wait_ge(set_up, SET_UP)
            def roots(n, c, v_done, r_done):
                pool.wait_ge(v_done, n + 1)
                nc.gpsimd.tensor_tensor(rstd[c][:, :], moments[c][:, :, 1], eps[:, :], ALU.add).then_inc(r_done, 1)
                pool.wait_ge(r_done, 2 * n + 1)
                nc.gpsimd.tensor_tensor(rstd[c][:, :], rstd[c][:, :], exponent[:, :], ALU.pow).then_inc(r_done, 1)

            def scale(n, c, b):
                pool.wait_ge(o_loaded[c], 64 * b + 64)
                nc.gpsimd.tensor_tensor(oc[c][:, :, :], oc[c][:, :, :], recb[c][:, :, :], ALU.mult).then_inc(scaled, 1)

            def place_values(n, c, b):
                nc.gpsimd.tensor_copy(v_now[c][:, :], v_all[:, b, :]).then_inc(v_placed, 1)
                nc.gpsimd.tensor_copy(mask_now[c][:, :], mask[:, bass.ds(n * TT, TT)]).then_inc(mask_placed, 1)

            def mask_and_keep(n, c):
                pool.wait_ge(mask_placed, n + 1)
                pool.wait_ge(normed, TT * (n + 1))
                nc.gpsimd.tensor_tensor(x1m[c][:, :, :], x1[c][:, :, :],
                                        mask_now[c][:, :].unsqueeze(2).to_broadcast([P, TT, D]),
                                        ALU.mult).then_inc(masked, 1)
                nc.gpsimd.tensor_copy(x2_all[:, bass.ds(n * TT, TT), :], x1[c][:, :, :]).then_inc(kept, 1)

            def place(n, c):
                pool.wait_ge(normed2, TT * (n + 1))
                nc.gpsimd.tensor_copy(x2_all[:, bass.ds(n * TT, TT), :], x2[c][:, :, :]).then_inc(placed, 1)

            def first():
                scale(0, 0, 0)
                place_values(0, 0, 0)
                roots(0, 0, var_done, rstd_done)
                mask_and_keep(0, 0)

            def slot(n, c, b, before=True, after=True):
                if before:
                    scale(n + 1, 1 - c, b + c)
                if after:
                    roots(n - 1, 1 - c, var2_done, rstd2_done)
                if before:
                    place_values(n + 1, 1 - c, b + c)
                if after:
                    place(n - 1, 1 - c)
                if before:
                    roots(n + 1, 1 - c, var_done, rstd_done)
                    mask_and_keep(n + 1, 1 - c)

            def last():
                roots(NCH - 1, 1, var2_done, rstd2_done)
                place(NCH - 1, 1)

            chunks(pool, first, slot, last)


NT = T * 2 // P + E_
FAC = 3 * D + 3 * HID
U32 = mybir.dt.uint32


def route_and_merge(nc, io, x2_all, logits, weights, rows, token_of, tile_expert, w1, w3, w2, b13, ident):
    with ExitStack() as ctx:
        def sb(name, shape, dt=F32):
            return ctx.enter_context(nc.sbuf_tensor("ro_" + name, shape, dt))

        def sem(name):
            return ctx.enter_context(nc.semaphore("ro_" + name))

        tri = sb("tri", [P, P])
        ones = sb("ones", [P, P])
        order = sb("order", [P, E_])
        slots = sb("slots", [P, NT])
        lanes = sb("lanes", [P, P])
        tokens = sb("tokens", [P, NTT])
        PIECE = NTT // 8
        lane_hot = [sb(f"lane_hot{i}", [P, PIECE, P]) for i in range(2)]
        slot_hot = [sb(f"slot_hot{i}", [P, PIECE, NT]) for i in range(2)]
        place_i = sb("place_i", [P, 2, 2, NTT], I32)
        slot, lane = sb("slot", [P, 2, NTT]), sb("lane", [P, 2, NTT])
        factors = [sb(f"factors{i}", [P, FAC]) for i in range(2)]
        first, second, equal, key, rest, total, run, run2 = (
            sb(n, [P, NTT, E_]) for n in ("first", "second", "equal", "key", "rest", "total", "run", "run2"))
        top1, top2, best, e2 = (sb(n, [P, NTT]) for n in ("top1", "top2", "best", "e2"))
        count_i = sb("count_i", [P, 2, E_], I32)
        tiles, ends, ends2 = (sb(n, [P, E_]) for n in ("tiles", "ends", "ends2"))
        place = sb("place", [P, 2, NTT])
        passed = sb("passed", [1, NT, E_])
        owner = sb("owner", [1, NT])
        ps_c = [ctx.enter_context(nc.psum_tensor(f"ro_c{i}", [P, NTT, E_], F32)) for i in range(2)]
        ps_m = [ctx.enter_context(nc.psum_tensor(f"ro_m{i}", [P, HID], F32)) for i in range(6)]
        const_loaded, w_loaded, bias_loaded = sem("const_loaded"), sem("w_loaded"), sem("bias_loaded")
        factors_loaded = [sem(f"factors_loaded{i}") for i in range(2)]
        chosen, counted, exp_done, steps = sem("chosen"), sem("counted"), sem("exp_done"), sem("steps")
        difference, hot, reversed_, x2_stored = sem("difference"), sem("hot"), sem("reversed"), sem("x2_stored")
        valued = sem("valued")
        low_rank, merged, cleared = sem("low_rank"), sem("merged"), sem("cleared")
        block = ctx.enter_context(nc.Block())

        @block.sync
        def _(sp):
            for dst, name in ((tri, "tri"), (ones, "all_ones"), (order, "order"), (slots, "slots"),
                              (lanes, "lanes"), (tokens, "tokens")):
                sp.dma_start(dst[:, :], io[name]).then_inc(const_loaded, 16)
            for i in range(2):
                sp.wait_ge(cleared, i + 1)
                sp.dma_start(factors[i][0:R, :], io["factors"][i]).then_inc(factors_loaded[i], 16)
            sp.dma_start(io["x2_rows"].rearrange("(t p) d -> p t d", p=P), x2_all[:, :, :]).then_inc(x2_stored, 16)
            for dst, name in ((w1, "w1T"), (w3, "w3T"), (w2, "w2T")):
                sp.dma_start(dst[:, :, :, :], io[name].rearrange("e (k p) n -> p e k n", p=P)).then_inc(w_loaded, 16)
            sp.dma_start(b13[:, :, :, :].rearrange("p e a h -> p (e a h)"),
                         bass.AP(io["b13"].tensor, 0, [[0, P], [1, E_ * 2 * HID]])).then_inc(bias_loaded, 16)
            sp.dma_start(ident[:, :], io["ident"]).then_inc(bias_loaded, 16)
            with sp.Fori(0, E_ // 2 - 1) as pair:
                for i in range(2):
                    sp.wait_ge(low_rank, 6 * (2 * pair + i) + 6)
                    sp.dma_start(factors[i][0:R, :], io["factors"][2 * pair + i + 2]).then_inc(factors_loaded[i], 16)
            sp.wait_ge(bias_loaded, 32)
            sp.wait_ge(x2_stored, 16)

        @block.tensor
        def _(pe):
            pe.sem_inc(merged, 6)
            pe.wait_ge(const_loaded, 96)
            pe.wait_ge(chosen, 1)
            nc.tensor.matmul(ps_c[0][:, :, :], tri[:, :], equal[:, :, :], start=True, stop=True)
            nc.tensor.matmul(ps_c[1][:, :, :], ones[:, :], equal[:, :, :], start=True, stop=True).then_inc(counted, 1)
            into = ps_c[0][:, :, :].rearrange("p t e -> p (t e)")[:, 0:NT]
            for piece in range(2 * NTT // PIECE):
                pe.wait_ge(hot, piece + 1)
                pe.wait_ge(valued, piece + 1)
                for t in range(PIECE):
                    last = nc.tensor.matmul(into, lane_hot[piece % 2][:, t, :], slot_hot[piece % 2][:, t, :],
                                            start=(piece == 0 and t == 0), stop=(piece == 2 * NTT // PIECE - 1 and t == PIECE - 1))
                last.then_inc(reversed_, 1)
            with pe.Fori(0, E_ // 2) as pair:
                for i in range(2):
                    pe.wait_ge(factors_loaded[i], 16 * pair + 16)
                    f = factors[i]
                    for n in range(6):
                        pe.wait_ge(merged, 6 * (2 * pair + i) + n + 1)
                        out = ps_m[n]
                        if n < 4:
                            a, b = (n // 2) * D + (n % 2) * P, 3 * D + (n // 2) * HID
                            last = nc.tensor.matmul(out[:, :], f[:, a:a + P], f[:, b:b + HID], start=True, stop=True)
                        else:
                            for m in range(2):
                                a = 3 * D + 2 * HID + (2 * (n - 4) + m) * P
                                last = nc.tensor.matmul(out[:, m * D:(m + 1) * D], f[:, a:a + P],
                                                        f[:, 2 * D:3 * D], start=True, stop=True)
                        last.then_inc(low_rank, 1)

        @block.scalar
        def _(act):
            act.wait_ge(difference, 1)
            nc.scalar.activation(e2[:, :], top2[:, :], ACT.Exp).then_inc(exp_done, 1)

        @block.vector
        def _(dve):
            done = [0]

            def step(instruction):
                done[0] += 1
                instruction.then_inc(steps, 1)
                dve.wait_ge(steps, done[0])

            def over_experts(a):
                return a.unsqueeze(2).to_broadcast([P, NTT, E_])

            def over_tiles(a):
                return a.unsqueeze(1).to_broadcast([P, NTT, E_])

            def pick(values, top, onehot):
                step(nc.vector.tensor_reduce(top, values, AXX, ALU.max))
                step(nc.vector.tensor_tensor(equal[:, :, :], values, over_experts(top), ALU.is_equal))
                step(nc.vector.tensor_tensor(key[:, :, :], equal[:, :, :], over_tiles(order[:, :]), ALU.mult))
                step(nc.vector.tensor_reduce(best[:, :], key[:, :, :], AXX, ALU.max))
                step(nc.vector.tensor_tensor(onehot, key[:, :, :], over_experts(best[:, :]), ALU.is_equal))

            dve.wait_ge(const_loaded, 96)
            pick(logits[:, :, :], top1[:, :], first[:, :, :])
            step(nc.vector.scalar_tensor_tensor(out=rest[:, :, :], in0=first[:, :, :], scalar=-3e38,
                                                in1=logits[:, :, :], op0=ALU.mult, op1=ALU.add))
            pick(rest[:, :, :], top2[:, :], second[:, :, :])
            nc.vector.tensor_tensor(equal[:, :, :], first[:, :, :], second[:, :, :], ALU.add).then_inc(chosen, 1)
            nc.vector.tensor_tensor(top2[:, :], top2[:, :], top1[:, :], ALU.subtract).then_inc(difference, 1)
            dve.wait_ge(exp_done, 1)
            step(nc.vector.tensor_scalar(best[:, :], e2[:, :], 1.0, None, ALU.add))
            step(nc.vector.reciprocal(weights[:, 0, :], best[:, :]))
            step(nc.vector.tensor_tensor(weights[:, 1, :], e2[:, :], weights[:, 0, :], ALU.mult))
            dve.wait_ge(counted, 1)
            step(nc.vector.tensor_copy(total[:, :, :], ps_c[1][:, :, :]))
            src, dst = total, run
            for shift in (1, 2, 4, 8, 16):
                nc.vector.tensor_copy(dst[:, 0:shift, :], src[:, 0:shift, :])
                step(nc.vector.tensor_tensor(dst[:, shift:, :], src[:, shift:, :], src[:, :NTT - shift, :], ALU.add))
                src, dst = dst, (run2 if dst is run else run)
            step(nc.vector.tensor_scalar(count_i[:, 0, :], src[:, NTT - 1, :], float(P - 1), None, ALU.add))
            step(nc.vector.tensor_scalar(count_i[:, 1, :], count_i[:, 0, :], 7, None, ALU.arith_shift_right))
            step(nc.vector.tensor_copy(tiles[:, :], count_i[:, 1, :]))
            a, b = tiles, ends
            for shift in (1, 2, 4):
                nc.vector.tensor_copy(b[:, 0:shift], a[:, 0:shift])
                step(nc.vector.tensor_tensor(b[:, shift:], a[:, shift:], a[:, :E_ - shift], ALU.add))
                a, b = b, (ends2 if b is ends else ends)
            last_tile = a
            step(nc.vector.tensor_tensor(b[:, :], last_tile[:, :], tiles[:, :], ALU.subtract))
            step(nc.vector.tensor_scalar(b[:, :], b[:, :], float(P), None, ALU.mult))
            step(nc.vector.tensor_tensor(key[:, :, :], src[:, :, :], total[:, :, :], ALU.subtract))
            step(nc.vector.tensor_tensor(key[:, :, :], ps_c[0][:, :, :], key[:, :, :], ALU.add))
            step(nc.vector.tensor_tensor(key[:, :, :], key[:, :, :], over_tiles(b[:, :]), ALU.add))
            for n, onehot in enumerate((first, second)):
                step(nc.vector.tensor_tensor(rest[:, :, :], key[:, :, :], onehot[:, :, :], ALU.mult))
                step(nc.vector.tensor_reduce(place[:, n, :], rest[:, :, :], AXX, ALU.add))
            step(nc.vector.tensor_copy(rows[:, :, :], place[:, :, :]))
            step(nc.vector.tensor_copy(place_i[:, 0, :, :], place[:, :, :]))
            step(nc.vector.tensor_scalar(place_i[:, 1, :, :], place_i[:, 0, :, :], 7, None, ALU.arith_shift_right))
            step(nc.vector.tensor_copy(slot[:, :, :], place_i[:, 1, :, :]))
            step(nc.vector.scalar_tensor_tensor(out=lane[:, :, :], in0=slot[:, :, :], scalar=-float(P),
                                                in1=place[:, :, :], op0=ALU.mult, op1=ALU.add))
            for piece in range(2 * NTT // PIECE):
                n, cut, i = piece // 8, slice(piece % 8 * PIECE, (piece % 8 + 1) * PIECE), piece % 2
                if piece >= 2:
                    dve.wait_ge(reversed_, piece - 1)
                nc.vector.tensor_tensor(lane_hot[i][:, :, :], lane[:, n, cut].unsqueeze(2).to_broadcast([P, PIECE, P]),
                                        lanes[:, :].unsqueeze(1).to_broadcast([P, PIECE, P]),
                                        ALU.is_equal)
                nc.vector.tensor_tensor(slot_hot[i][:, :, :], slot[:, n, cut].unsqueeze(2).to_broadcast([P, PIECE, NT]),
                                        slots[:, :].unsqueeze(1).to_broadcast([P, PIECE, NT]),
                                        ALU.is_equal).then_inc(hot, 1)
            step(nc.vector.tensor_tensor(passed[:, :, :], slots[0:1, :].unsqueeze(2).to_broadcast([1, NT, E_]),
                                         last_tile[0:1, :].unsqueeze(1).to_broadcast([1, NT, E_]), ALU.is_ge))
            step(nc.vector.tensor_reduce(owner[:, :], passed[:, :, :], AXX, ALU.add))
            step(nc.vector.tensor_scalar(owner[:, :], owner[:, :], float(E_ - 1), None, ALU.min))
            step(nc.vector.tensor_copy(tile_expert[:, :], owner[:, :]))
            dve.wait_ge(reversed_, 2 * NTT // PIECE)
            step(nc.vector.tensor_copy(token_of[:, :],
                                       ps_c[0][:, :, :].rearrange("p t e -> p (t e)")[:, 0:NT]))

            dve.wait_ge(w_loaded, 48)
            with dve.Fori(0, E_) as e:
                for n in range(6):
                    target = (w1, w3, w2)[n // 2]
                    if n < 4:
                        into = target[:, e, n % 2, :]
                    else:
                        into = target[:, e, 2 * (n - 4):2 * (n - 4) + 2, :].rearrange("p a d -> p (a d)")
                    dve.wait_ge(low_rank, 6 * e + n + 1)
                    nc.vector.tensor_tensor(into, ps_m[n][:, :], into, ALU.add).then_inc(merged, 1)

        @block.gpsimd
        def _(pool):
            for i in range(2):
                nc.gpsimd.memset(factors[i][:, :], 0.0).then_inc(cleared, 1)
            pool.wait_ge(const_loaded, 96)
            for piece in range(2 * NTT // PIECE):
                cut, i = slice(piece % 8 * PIECE, (piece % 8 + 1) * PIECE), piece % 2
                pool.wait_ge(hot, piece + 1)
                nc.gpsimd.tensor_tensor(slot_hot[i][:, :, :], slot_hot[i][:, :, :],
                                        tokens[:, cut].unsqueeze(2).to_broadcast([P, PIECE, NT]),
                                        ALU.mult).then_inc(valued, 1)


def experts(nc, io, token_of, tile_expert, w1, w3, w2, b13, ident):
    with ExitStack() as ctx:
        def sb(name, shape, dt=F32):
            return ctx.enter_context(nc.sbuf_tensor("xp_" + name, shape, dt))

        def sem(name):
            return ctx.enter_context(nc.semaphore("xp_" + name))

        KH = HID // P
        b2 = sb("b2", [P, E_, D])
        b2_loaded = sem("b2_loaded")
        x = [sb(f"x{i}", [P, D]) for i in range(2)]
        xT = [sb(f"xT{i}", [P, KT, P]) for i in range(2)]
        h = [sb(f"h{i}", [P, 2, HID]) for i in range(2)]
        g = [sb(f"g{i}", [P, HID]) for i in range(2)]
        gT = [sb(f"gT{i}", [P, KH, P]) for i in range(2)]
        y = [sb(f"y{i}", [P, D]) for i in range(2)]
        ps_h = [ctx.enter_context(nc.psum_tensor(f"xp_ps_h{i}", [P, 2, HID], F32)) for i in range(2)]
        ps_x = ctx.enter_context(nc.psum_tensor("xp_ps_x", [P, KT, P], F32))
        ps_g = ctx.enter_context(nc.psum_tensor("xp_ps_g", [P, KH, P], F32))
        ps_y = ctx.enter_context(nc.psum_tensor("xp_ps_y", [P, 512], F32))
        x_loaded = [sem(f"x_loaded{i}") for i in range(2)]
        y_stored = [sem(f"y_stored{i}") for i in range(2)]
        (x_turned, x_copied, h_ready, biased, silu_done, g_done, g_turned, g_copied, y_ready, y_done) = (
            sem(n) for n in ("x_turned", "x_copied", "h_ready", "biased", "silu_done", "g_done", "g_turned",
                             "g_copied", "y_ready", "y_done"))
        block = ctx.enter_context(nc.Block())

        LOOPED = NT - 4

        def pipeline(eng, head, body, tail):
            head()
            with eng.Fori(0, LOOPED // 2) as pair:
                for i in range(2):
                    body(2 * pair + 1 + i, 1 + i)
            tail()

        @block.sync
        def _(sp):
            sp.dma_start(b2[:, :, :].rearrange("p e d -> p (e d)"),
                         bass.AP(io["b2"].tensor, 0, [[0, P], [1, E_ * D]])).then_inc(b2_loaded, 16)

            def store(s, parity):
                sp.wait_ge(y_done, 1 + s + 1)
                sp.dma_start(io["table_y"][bass.ds(s * P, P), :], y[parity % 2][:, :]).then_inc(y_stored[parity % 2], 16)

            with sp.Fori(0, (NT - 4) // 2) as pair:
                for i in range(2):
                    store(2 * pair + i, i)
            for s in range(NT - 4, NT):
                store(s, s)
            for i in range(2):
                sp.wait_ge(y_stored[i], 1 + 16 * NT // 2)

        @block.gpsimd
        def _(pool):
            for s in range(NT):
                if s >= 2:
                    pool.wait_ge(x_turned, s - 1)
                pool.indirect_dma_start(out=x[s % 2][:, :], out_offset=None, in_=io["x2_rows"],
                                        in_offset=bass.IndirectOffsetOnAxis(token_of[:, s:s + 1], 0)
                                        ).then_inc(x_loaded[s % 2], 16)

        @block.tensor
        def _(pe):
            pe.sem_inc(y_done, 1)

            def turn_x(s, parity, pair):
                pe.wait_ge(x_loaded[parity % 2], 16 * pair + 16)
                pe.wait_ge(x_copied, s)
                for k in range(KT):
                    last = nc.tensor.transpose(ps_x[:, k, :], x[parity % 2][:, k * P:(k + 1) * P], ident[:, :])
                last.then_inc(x_turned, 1)

            def hidden(s, parity):
                e = pe.value_load(tile_expert[0:1, bass.ds(s, 1)], min_val=0, max_val=E_ - 1)
                pe.wait_ge(x_copied, s + 1)
                for n, w in enumerate((w1, w3)):
                    for k in range(KT):
                        last = nc.tensor.matmul(ps_h[parity % 2][:, n, :], xT[parity % 2][:, k, :], w[:, e, k, :],
                                                start=(k == 0), stop=(k == KT - 1))
                last.then_inc(h_ready, 1)

            def turn_g(s, parity):
                pe.wait_ge(g_done, s + 1)
                pe.wait_ge(g_copied, s)
                for k in range(KH):
                    last = nc.tensor.transpose(ps_g[:, k, :], g[parity % 2][:, k * P:(k + 1) * P], ident[:, :])
                last.then_inc(g_turned, 1)

            def out(s, parity):
                e = pe.value_load(tile_expert[0:1, bass.ds(s, 1)], min_val=0, max_val=E_ - 1)
                pe.wait_ge(g_copied, s + 1)
                pe.wait_ge(y_done, 1 + s)
                for k in range(KH):
                    last = nc.tensor.matmul(ps_y[:, 0:D], gT[parity % 2][:, k, :], w2[:, e, k, :],
                                            start=(k == 0), stop=(k == KH - 1))
                last.then_inc(y_ready, 1)

            def head():
                turn_x(0, 0, 0)
                hidden(0, 0)
                turn_x(1, 1, 0)
                hidden(1, 1)
                turn_x(2, 0, 1)
                turn_g(0, 0)

            def body(s, parity):
                hidden(s + 1, parity + 1)
                turn_x(s + 2, parity, pair_of(s, parity))
                turn_g(s, parity)
                out(s - 1, parity - 1)

            def pair_of(s, parity):
                return s // 2 + 1

            def tail():
                for s in range(NT - 3, NT):
                    if s + 1 < NT:
                        hidden(s + 1, s + 1)
                    if s + 2 < NT:
                        turn_x(s + 2, s, (s + 2) // 2)
                    turn_g(s, s)
                    out(s - 1, s - 1)
                out(NT - 1, NT - 1)

            pipeline(pe, head, body, tail)

        @block.scalar
        def _(act):
            def copy_x(s, parity):
                act.wait_ge(x_turned, s + 1)
                nc.scalar.activation(xT[parity % 2][:, :, :], ps_x[:, :, :], ACT.Copy).then_inc(x_copied, 1)

            def copy_g(s, parity):
                act.wait_ge(g_turned, s + 1)
                nc.scalar.activation(gT[parity % 2][:, :, :], ps_g[:, :, :], ACT.Copy).then_inc(g_copied, 1)

            def silu(s, parity):
                act.wait_ge(biased, s + 1)
                nc.scalar.activation(h[parity % 2][:, 0, :], h[parity % 2][:, 0, :], ACT.Silu).then_inc(silu_done, 1)

            def head():
                copy_x(0, 0)
                copy_x(1, 1)
                silu(0, 0)
                copy_x(2, 0)
                copy_g(0, 0)
                silu(1, 1)

            def body(s, parity):
                copy_x(s + 2, parity)
                copy_g(s, parity)
                silu(s + 1, parity + 1)

            def tail():
                for s in range(NT - 3, NT):
                    if s + 2 < NT:
                        copy_x(s + 2, s)
                    copy_g(s, s)
                    if s + 1 < NT:
                        silu(s + 1, s + 1)

            pipeline(act, head, body, tail)

        @block.vector
        def _(dve):
            for i in range(2):
                dve.sem_inc(y_stored[i], 1)

            def gate(s, parity):
                i = parity % 2
                e = dve.value_load(tile_expert[0:1, bass.ds(s, 1)], min_val=0, max_val=E_ - 1)
                dve.wait_ge(h_ready, s + 1)
                nc.vector.tensor_tensor(h[i][:, :, :], ps_h[i][:, :, :], b13[:, e, :, :], ALU.add).then_inc(biased, 1)
                dve.wait_ge(silu_done, s + 1)
                nc.vector.tensor_tensor(g[i][:, :], h[i][:, 0, :], h[i][:, 1, :], ALU.mult).then_inc(g_done, 1)

            def out(s, parity):
                i = parity % 2
                e = dve.value_load(tile_expert[0:1, bass.ds(s, 1)], min_val=0, max_val=E_ - 1)
                dve.wait_ge(y_ready, s + 1)
                dve.wait_ge(y_stored[i], 1 + stored_before(s, parity))
                nc.vector.tensor_tensor(y[i][:, :], ps_y[:, 0:D], b2[:, e, :], ALU.add).then_inc(y_done, 1)

            def stored_before(s, parity):
                return 16 * (s // 2)

            def head():
                gate(0, 0)
                gate(1, 1)
                dve.wait_ge(b2_loaded, 16)

            def body(s, parity):
                gate(s + 1, parity + 1)
                out(s - 1, parity - 1)

            def tail():
                for s in range(NT - 3, NT):
                    if s + 1 < NT:
                        gate(s + 1, s + 1)
                    out(s - 1, s - 1)
                out(NT - 1, NT - 1)

            pipeline(dve, head, body, tail)


def combine(nc, io, x2_all, weights, rows):
    with ExitStack() as ctx:
        def sb(name, shape, dt=F32):
            return ctx.enter_context(nc.sbuf_tensor("co_" + name, shape, dt))

        def sem(name):
            return ctx.enter_context(nc.semaphore("co_" + name))

        ya = [sb(f"ya{i}", [P, TT, D]) for i in range(2)]
        yb = [sb(f"yb{i}", [P, TT, D]) for i in range(2)]
        out = [sb(f"out{i}", [P, TT, D]) for i in range(2)]
        stats = [sb(f"stats{i}", [P, TT, 6]) for i in range(2)]
        moments = [sb(f"moments{i}", [P, TT, 4]) for i in range(2)]
        rstd = [sb(f"rstd{i}", [P, TT]) for i in range(2)]
        exponent = sb("exponent", [P, TT])
        eps = sb("eps", [P, TT])
        gathered = [sem(f"gathered{i}") for i in range(2)]
        exponent_set, halves_done, partial, summed, stat_done, var_done, rstd_done, normed = (
            sem(n) for n in ("exponent_set", "halves_done", "partial", "summed", "stat_done", "var_done", "rstd_done", "normed"))
        stored = [sem(f"stored{i}") for i in range(2)]
        block = ctx.enter_context(nc.Block())

        @block.gpsimd
        def _(pool):
            def gather(c):
                if c >= 2:
                    pool.wait_ge(summed, TT * (c - 1))
                for t in range(TT):
                    for n, dst in enumerate((ya, yb)):
                        pool.indirect_dma_start(
                            out=dst[c % 2][:, t, :], out_offset=None, in_=io["table_y"],
                            in_offset=bass.IndirectOffsetOnAxis(rows[:, n, c * TT + t:c * TT + t + 1], 0)
                        ).then_inc(gathered[c % 2], 16)

            gather(0)
            for c in range(NCH):
                if c + 1 < NCH:
                    gather(c + 1)
                pool.wait_ge(var_done, c + 1)
                nc.gpsimd.tensor_tensor(rstd[c % 2][:, :], moments[c % 2][:, :, 1], eps[:, :], ALU.add).then_inc(rstd_done, 1)
                if c == 0:
                    pool.wait_ge(exponent_set, 2)
                pool.wait_ge(rstd_done, 2 * c + 1)
                nc.gpsimd.tensor_tensor(rstd[c % 2][:, :], rstd[c % 2][:, :], exponent[:, :], ALU.pow).then_inc(rstd_done, 1)

        @block.vector
        def _(dve):
            for i in range(2):
                dve.sem_inc(stored[i], 1)
            nc.vector.memset(exponent[:, :], -0.5).then_inc(exponent_set, 1)
            nc.vector.memset(eps[:, :], EPS).then_inc(exponent_set, 1)

            def add_up(pair, i):
                c = 2 * pair + i
                dve.wait_ge(gathered[i], 16 * 2 * TT * (pair + 1))
                for t in range(TT):
                    n = c * TT + t
                    nc.vector.scalar_tensor_tensor(out=ya[i][:, t, :], in0=ya[i][:, t, :],
                                                   scalar=weights[:, 0, bass.ds(n, 1)], in1=x2_all[:, n, :],
                                                   op0=ALU.mult, op1=ALU.add).then_inc(partial, 1)
                for t in range(TT):
                    n = c * TT + t
                    dve.wait_ge(partial, n + 1)
                    if t == 0:
                        dve.wait_ge(stored[i], 1 + 16 * pair)
                    nc.vector.scalar_tensor_tensor(out=out[i][:, t, :], in0=yb[i][:, t, :],
                                                   scalar=weights[:, 1, bass.ds(n, 1)], in1=ya[i][:, t, :],
                                                   op0=ALU.mult, op1=ALU.add).then_inc(summed, 1)
                for t in range(TT):
                    dve.wait_ge(summed, c * TT + t + 1)
                    nc.vector.bn_stats(stats[i][:, t, :], out[i][:, t, :]).then_inc(stat_done, 1)
                moments_of(dve, nc, stat_done, c * TT + TT, stats[i], moments[i], halves_done, 4 * c, var_done)

            def normalise(pair, i):
                c = 2 * pair + i
                dve.wait_ge(rstd_done, 2 * c + 2)
                for t in range(TT):
                    nc.vector.tensor_scalar(out[i][:, t, :], out[i][:, t, :], moments[i][:, t, 0:1],
                                            rstd[i][:, t:t + 1], ALU.subtract, ALU.mult).then_inc(normed, 1)

            with dve.Fori(0, NCH // 2) as pair:
                for i in range(2):
                    add_up(pair, i)
                    normalise(pair, i)

        @block.sync
        def _(sp):
            with sp.Fori(0, NCH // 2) as pair:
                for i in range(2):
                    c = 2 * pair + i
                    sp.wait_ge(normed, TT * (c + 1))
                    sp.dma_start(io["out"][bass.ds(c * CH, CH), :].rearrange("(t p) d -> p t d", p=P),
                                 out[i][:, :, :]).then_inc(stored[i], 16)
            for i in range(2):
                sp.wait_ge(stored[i], 1 + 16 * NCH // 2)


def decoder_layer(nc, io):
    def scratch(name, shape, dt=F32):
        io[name] = nc.dram_tensor(name, shape, dt).ap()

    scratch("line", [H, 2 * S])
    scratch("strips", [P, H, STRIP])
    scratch("qstack", [2, (ROWS + 1) * 8, T], BF16)
    scratch("kstack", [2, (ROWS + 1) * 8, T], BF16)
    scratch("vpad", [T, H * 32])
    scratch("kmax", [P, 1])
    scratch("oT", [HG, P, T])
    scratch("rec", [H, T])
    scratch("x2_rows", [T, D])
    scratch("table_y", [NT * P, D])
    io["out"] = io["out"].rearrange("b s d -> (b s) d")
    position_tables(nc, io)
    with nc.sbuf_tensor("bias_strips", [P, HG, HPG, STRIP], F32) as strips:
        project_qkv(nc, io, strips)
        self_attention(nc, io, strips)
        check_and_exact_attention(nc, io, strips)
    with ExitStack() as ctx:
        def sb(name, shape, dt=F32):
            return ctx.enter_context(nc.sbuf_tensor(name, shape, dt))

        x2_all = sb("x2_all", [P, NTT, D])
        logits = sb("logits", [P, NTT, E_])
        cross_block(nc, io, x2_all, logits)
        weights = sb("weights", [P, 2, NTT])
        rows = sb("rows", [P, 2, NTT], U32)
        token_of = sb("token_of", [P, NT], U32)
        tile_expert = sb("tile_expert", [1, NT], I32)
        with ExitStack() as inner:
            w1 = inner.enter_context(nc.sbuf_tensor("w1", [P, E_, KT, HID], F32))
            w3 = inner.enter_context(nc.sbuf_tensor("w3", [P, E_, KT, HID], F32))
            w2 = inner.enter_context(nc.sbuf_tensor("w2", [P, E_, HID // P, D], F32))
            b13 = inner.enter_context(nc.sbuf_tensor("ffn_b13", [P, E_, 2, HID], F32))
            ident = inner.enter_context(nc.sbuf_tensor("ffn_ident", [P, P], F32))
            route_and_merge(nc, io, x2_all, logits, weights, rows, token_of, tile_expert, w1, w3, w2,
                            b13, ident)
            experts(nc, io, token_of, tile_expert, w1, w3, w2, b13, ident)
        combine(nc, io, x2_all, weights, rows)


def constants():
    dist = np.abs(np.arange(2 * S) - (S - 1)).astype(np.float32)
    index = np.clip(np.round(dist / np.float32(S - 1) * np.float32(RES - 1)).astype(np.int32), 0, RES - 1)
    proto = np.linspace(0.0, 1.0, RES).astype(np.float32)
    ramp = np.zeros((TAPS, RES), np.float32)
    for tap in range(TAPS):
        ramp[tap, tap:] = proto[:RES - tap]
    p = np.arange(P)
    return {
        "onehot": (np.arange(RES)[:, None] == index[None, :]).astype(np.float32),
        "ramp": ramp,
        "ident": np.eye(P, dtype=np.float32),
        "block8": (p[:, None] // HD == np.arange(8)[None, :]).astype(np.float32),
        "members": (p[:, None] % 8 == np.arange(8)[None, :]).astype(mybir.dt.np(BF16)),
        "tri": (p[:, None] < p[None, :]).astype(np.float32),
        "all_ones": np.ones((P, P), np.float32),
        "order": np.tile(np.arange(E_, 0, -1, dtype=np.float32), (P, 1)),
        "slots": np.tile(np.arange(NT, dtype=np.float32), (P, 1)),
        "lanes": np.tile(np.arange(P, dtype=np.float32), (P, 1)),
        "tokens": np.arange(T, dtype=np.float32).reshape(NTT, P).T,
    }


def laid_out(x, ctx_768, mask_BxS_bk0, L0_attn_Wqkv, L0_attn_Wout, L0_attn_Wpos, L0_attn_coeffs, L0_xattn_Wq,
             L0_xattn_Wkv, L0_ffn_Wg, L0_ffn_W1, L0_ffn_b1, L0_ffn_A1, L0_ffn_B1, L0_ffn_W2, L0_ffn_b2, L0_ffn_A2,
             L0_ffn_B2, L0_ffn_W3, L0_ffn_b3, L0_ffn_A3, L0_ffn_B3):
    def turned(w):
        return w.transpose(0, 2, 1)

    by_dim = np.arange(D).reshape(2, 8, HD).transpose(0, 2, 1).ravel()
    order = np.concatenate([by_dim, D + by_dim, 2 * D + np.arange(D)])
    xf = x.reshape(T, D)
    ctxT = ctx_768.reshape(B * NK, CD).T
    wkvT = L0_xattn_Wkv.T
    return {
        "x": xf, "xT": xf.T,
        "wqkvT": L0_attn_Wqkv[order].T, "coeffs": L0_attn_coeffs, "wposT": L0_attn_Wpos.T,
        "woutT": L0_attn_Wout.T, "wqT": L0_xattn_Wq.T, "wgT": L0_ffn_Wg.T,
        "ctxT_a": ctxT[:P], "ctxT_b": ctxT[P:], "wkvT_a": wkvT[:P], "wkvT_b": wkvT[P:],
        "mask": mask_BxS_bk0.reshape(NTT, P).T,
        "w1T": turned(L0_ffn_W1), "w3T": turned(L0_ffn_W3), "w2T": turned(L0_ffn_W2),
        "factors": np.concatenate([L0_ffn_A1, L0_ffn_A3, turned(L0_ffn_B2), turned(L0_ffn_B1), turned(L0_ffn_B3),
                                   L0_ffn_A2], axis=2),
        "b13": np.stack([L0_ffn_b1, L0_ffn_b3], axis=1), "b2": L0_ffn_b2,
    }


def kernel(**inputs):
    import concourse.bacc as bacc
    from concourse.bass_utils import run_bass_kernel_spmd

    nc = bacc.Bacc("TRN2", target_bir_lowering=False, num_devices=1)
    arrays, io = {}, {}
    for name, a in {**laid_out(**{k: np.asarray(v) for k, v in inputs.items()}), **constants()}.items():
        arrays[name] = np.ascontiguousarray(a)
        io[name] = nc.dram_tensor(name, a.shape, mybir.dt.from_np(a.dtype), kind="ExternalInput").ap()
    io["out"] = nc.dram_tensor("out", (B, S, D), F32, kind="ExternalOutput").ap()
    decoder_layer(nc, io)
    return run_bass_kernel_spmd(nc, [arrays], core_ids=[0]).results[0]["out"]
```
